# Optimizing a Trainium2 kernel written in Bass

```python
import numpy as np
import jax
import jax.numpy as jnp

def _softmax(x, axis=-1):
    return jax.nn.softmax(x, axis=axis)

def _gelu(x):
    return jax.nn.gelu(x, approximate=True)

def _silu(x):
    return jax.nn.silu(x)

def _sigmoid(x):
    return jax.nn.sigmoid(x)

def _layernorm(x, axis=-1, eps=1e-05):
    m = jnp.mean(x, axis=axis, keepdims=True)
    v = jnp.var(x, axis=axis, keepdims=True)
    return (x - m) / jnp.sqrt(v + eps)

def _scatter_add(tgt, idx, src, axis=0):
    return tgt.at[idx].add(src)

def _segment_sum(src, seg, n):
    return jax.ops.segment_sum(src, seg, n)
kernel_name = 'mk_gnn_preln_d2_gnn_r64_ed673e'

def setup_inputs(seed: int=0):
    np.random.seed(seed)
    _w = jnp.asarray

    def _rec_inputs():
        import jax
        import jax.numpy as jnp
        _gk = jax.random.key(seed)
        x = -8.776e-05 + 1 * jax.random.normal(jax.random.fold_in(_gk, 1), (50000, 256), jnp.float32)
        src = jax.random.randint(jax.random.fold_in(_gk, 2), (12500,), 0, 50000, jnp.int32)
        dst = jnp.minimum((50000 * jax.random.uniform(jax.random.fold_in(_gk, 3), (12500,)) ** 2.0).astype(jnp.int32), 49999)
        _o = jnp.argsort(dst, stable=True)
        src = src[_o]
        dst = dst[_o]
        edge_type_500 = jax.random.randint(jax.random.fold_in(_gk, 13), (12500,), 0, 500, jnp.int32)
        return (x, src, dst, edge_type_500)
    x, src, dst, edge_type_500 = _rec_inputs()

    def _L0_gnn_setup():
        import jax, jax.numpy as jnp
        import numpy as np
        N_NODES = 20000
        N_EDGES = 5000
        D = 256
        N_LAYERS = 3
        BN_EPS = 1e-05
        key = jax.random.key(seed)
        ks = jax.random.split(key, 5)
        x = jax.random.normal(ks[0], (N_NODES, D), dtype=jnp.float32)
        src = jax.random.randint(ks[1], (N_EDGES,), 0, N_NODES)
        dst = jax.random.randint(ks[2], (N_EDGES,), 0, N_NODES)
        scale = 1.0 / np.sqrt(D)
        thetas = jax.random.normal(ks[3], (N_LAYERS, D, D), dtype=jnp.float32) * scale
        phis = jax.random.normal(ks[4], (N_LAYERS, D, D), dtype=jnp.float32) * scale
        gammas = jnp.ones((N_LAYERS, D), dtype=jnp.float32)
        betas = jnp.zeros((N_LAYERS, D), dtype=jnp.float32)
        return {'x': x, 'src': src, 'dst': dst, 'thetas': thetas, 'phis': phis, 'gammas': gammas, 'betas': betas}
    _L0_gnn_all = _L0_gnn_setup()
    _L0_gnn_in = {k: v for k, v in _L0_gnn_all.items() if k in ('thetas', 'phis', 'gammas', 'betas')}
    del _L0_gnn_all

    def _L1_gnn_setup():
        import jax, jax.numpy as jnp
        import numpy as np
        G = (1.0, 1.0)

        def to_hypercomplex(x, n_blades):
            return x.reshape(*x.shape[:-1], n_blades, -1).swapaxes(-2, -1)

        def clifford_kernel_2d(w, g):
            g0, g1 = g
            k0 = jnp.concatenate([w[0], g0 * w[1], g1 * w[2], -g0 * g1 * w[3]], axis=1)
            k1 = jnp.concatenate([w[1], w[0], -g1 * w[3], g1 * w[2]], axis=1)
            k2 = jnp.concatenate([w[2], g0 * w[3], w[0], -g0 * w[1]], axis=1)
            k3 = jnp.concatenate([w[3], w[2], w[1], w[0]], axis=1)
            return jnp.concatenate([k0, k1, k2, k3], axis=0)

        def clifford_linear(x, w, b, g=G):
            N = x.shape[0]
            k = clifford_kernel_2d(w, g)
            xf = x.swapaxes(-2, -1).reshape(N, -1)
            out = xf @ k.T + b.reshape(-1)
            C_out = w.shape[1]
            return out.reshape(N, 4, C_out).swapaxes(-2, -1)
        key = jax.random.key(seed)
        ks = jax.random.split(key, 10)
        N, E, R, emb_dim = (100000, 9375, 500, 256)
        C = emb_dim // 4
        s = 0.05
        return {'h': jax.random.normal(ks[0], (N, emb_dim), jnp.float32), 'edge_index': jax.random.randint(ks[1], (2, E), 0, N, jnp.int64), 'edge_type': jax.random.randint(ks[2], (E,), 0, R, jnp.int64), 'relation_emb': jax.random.normal(ks[3], (R, emb_dim), jnp.float32), 'msg_w': jax.random.normal(ks[4], (4, C, C), jnp.float32) * s, 'msg_b': jax.random.normal(ks[5], (4, C), jnp.float32) * s, 'upd_w': jax.random.normal(ks[6], (4, C, C), jnp.float32) * s, 'upd_b': jax.random.normal(ks[7], (4, C), jnp.float32) * s, 'gate_w': jax.random.normal(ks[8], (1, emb_dim), jnp.float32) * s, 'gate_b': jax.random.normal(ks[9], (1,), jnp.float32) * s}
    _L1_gnn_all = _L1_gnn_setup()
    _L1_gnn_in = {k: v for k, v in _L1_gnn_all.items() if k in ('relation_emb', 'msg_w', 'msg_b', 'upd_w', 'upd_b', 'gate_w', 'gate_b')}
    del _L1_gnn_all
    return {'x': x, 'src': src, 'dst': dst, 'edge_type_500': edge_type_500, 'L0_gnn_thetas': _L0_gnn_in['thetas'], 'L0_gnn_phis': _L0_gnn_in['phis'], 'L0_gnn_gammas': _L0_gnn_in['gammas'], 'L0_gnn_betas': _L0_gnn_in['betas'], 'L1_gnn_relation_emb': _L1_gnn_in['relation_emb'], 'L1_gnn_msg_w': _L1_gnn_in['msg_w'], 'L1_gnn_msg_b': _L1_gnn_in['msg_b'], 'L1_gnn_upd_w': _L1_gnn_in['upd_w'], 'L1_gnn_upd_b': _L1_gnn_in['upd_b'], 'L1_gnn_gate_w': _L1_gnn_in['gate_w'], 'L1_gnn_gate_b': _L1_gnn_in['gate_b']}

def reference(x, src, dst, edge_type_500, L0_gnn_thetas, L0_gnn_phis, L0_gnn_gammas, L0_gnn_betas, L1_gnn_relation_emb, L1_gnn_msg_w, L1_gnn_msg_b, L1_gnn_upd_w, L1_gnn_upd_b, L1_gnn_gate_w, L1_gnn_gate_b):
    import jax
    import jax.numpy as jnp

    def _L0_gnn_ref(x, src, dst, thetas, phis, gammas, betas):
        import jax, jax.numpy as jnp
        import numpy as np
        N_NODES = 20000
        N_EDGES = 5000
        D = 256
        N_LAYERS = 3
        BN_EPS = 1e-05
        N = x.shape[0]
        for l in range(thetas.shape[0]):
            xi = x[src]
            xj = x[dst]
            e = jax.nn.relu((xj - xi) @ thetas[l].T + xi @ phis[l].T)
            agg = jax.ops.segment_max(e, src, num_segments=N)
            agg = jnp.where(agg < -1e+30, 0.0, agg)
            mu = agg.mean(axis=0)
            var = agg.var(axis=0)
            x = jax.nn.relu((agg - mu) * jax.lax.rsqrt(var + BN_EPS) * gammas[l] + betas[l])
        return x

    def _L1_gnn_ref(h, edge_index, edge_type, relation_emb, msg_w, msg_b, upd_w, upd_b, gate_w, gate_b):
        import jax, jax.numpy as jnp
        import numpy as np
        G = (1.0, 1.0)

        def to_hypercomplex(x, n_blades):
            return x.reshape(*x.shape[:-1], n_blades, -1).swapaxes(-2, -1)

        def clifford_kernel_2d(w, g):
            g0, g1 = g
            k0 = jnp.concatenate([w[0], g0 * w[1], g1 * w[2], -g0 * g1 * w[3]], axis=1)
            k1 = jnp.concatenate([w[1], w[0], -g1 * w[3], g1 * w[2]], axis=1)
            k2 = jnp.concatenate([w[2], g0 * w[3], w[0], -g0 * w[1]], axis=1)
            k3 = jnp.concatenate([w[3], w[2], w[1], w[0]], axis=1)
            return jnp.concatenate([k0, k1, k2, k3], axis=0)

        def clifford_linear(x, w, b, g=G):
            N = x.shape[0]
            k = clifford_kernel_2d(w, g)
            xf = x.swapaxes(-2, -1).reshape(N, -1)
            out = xf @ k.T + b.reshape(-1)
            C_out = w.shape[1]
            return out.reshape(N, 4, C_out).swapaxes(-2, -1)
        n_blades = 4
        num_nodes = h.shape[0]
        h_hc = to_hypercomplex(h, n_blades)
        r_hc = to_hypercomplex(relation_emb, n_blades)
        src, dst = (edge_index[0], edge_index[1])
        h_src = h_hc[src]
        r_uv = r_hc[edge_type]
        m = clifford_linear(h_src * r_uv, msg_w, msg_b)
        gate = jax.nn.sigmoid(r_uv.reshape(r_uv.shape[0], -1) @ gate_w.T + gate_b)
        m = m * gate[:, :, None]
        ones = jnp.ones_like(src, dtype=jnp.float32)
        deg_src = jax.ops.segment_sum(ones, src, num_segments=num_nodes)
        deg_dst = jax.ops.segment_sum(ones, dst, num_segments=num_nodes)
        norm = jnp.maximum(deg_src[src] * deg_dst[dst], 1.0) ** (-0.5)
        m = m * norm[:, None, None]
        h_agg = jax.ops.segment_sum(m, dst, num_segments=num_nodes)
        h_out = clifford_linear(h_hc + h_agg, upd_w, upd_b)
        return h_out.reshape(num_nodes, -1)
    edge_index = jnp.stack([src, dst])
    h = jnp.maximum(_layernorm(x, axis=-1), 0.0)
    x = x + _L0_gnn_ref(h, src, dst, L0_gnn_thetas, L0_gnn_phis, L0_gnn_gammas, L0_gnn_betas)
    h = jnp.maximum(_layernorm(x, axis=-1), 0.0)
    x = x + _L1_gnn_ref(h, edge_index, edge_type_500, L1_gnn_relation_emb, L1_gnn_msg_w, L1_gnn_msg_b, L1_gnn_upd_w, L1_gnn_upd_b, L1_gnn_gate_w, L1_gnn_gate_b)
    return x

_drawn_inputs = setup_inputs


def setup_inputs(seed=0):
    import zlib

    import numpy as np

    out = dict(_drawn_inputs(seed))
    spreads = {'L0_gnn_gammas': (1.0, 0.2), 'L0_gnn_betas': (0.0, 0.1)}
    factors = {'L1_gnn_msg_b': 8.0}
    for name, (base, spread) in spreads.items():
        noise = np.random.default_rng([zlib.crc32(name.encode()), seed]).standard_normal(out[name].shape)
        drawn = base * np.exp(spread * noise) if base else spread * noise
        out[name] = jnp.asarray(drawn.astype(out[name].dtype))
    for name, factor in factors.items():
        out[name] = (out[name] * factor).astype(out[name].dtype)
    return out
```

```python
import concourse.bass as bass
from concourse import mybir
from contextlib import ExitStack

F32 = mybir.dt.float32
BF16 = mybir.dt.bfloat16
I32 = mybir.dt.int32
ALU = mybir.AluOpType
ACT = mybir.ActivationFunctionType

P = 128
N = 50000
D = 256
E = 12500
R = 500
L = 3
TILES = 100
CHUNKS = TILES // 2
EP = TILES * P
CW = 2 * P
LAST = E // P
LASTN = E - LAST * P
LO = 256
PAD_KEY = 195 * LO + 255
CROW = EP
EPS = 1e-5
RT = 125

C_E, C_X, C_R, C_S, C_POS, C_KEY, SW = 0, 256, 512, 768, 769, 770, 776


class Program:
    pass


class Chain:

    def __init__(self, eng, sem):
        self.eng, self.sem, self.base, self.i, self.per, self.k = eng, sem, 0, 0, 0, 0

    def loop(self, i, per):
        self.base, self.i, self.per, self.k = self.base + self.k, i, per, 0

    def end(self, iters):
        assert self.k == self.per, (self.k, self.per)
        self.base, self.i, self.per, self.k = self.base + iters * self.per, 0, 0, 0

    def __call__(self, ins):
        ins.then_inc(self.sem, 1)
        self.k += 1
        self.eng.wait_ge(self.sem, self.i * self.per + (self.base + self.k))


class Signal:

    def __init__(self, sem, ahead):
        self.sem, self.ahead = sem, ahead

    def done(self, c):
        return c + (1 + self.ahead)

    def free(self, c, slots):
        assert self.ahead >= slots - 1
        return c + (1 + self.ahead - slots)


def staged(eng, total, slots, *steps, chain=None, counts=(), peel=0):
    ahead = max(a for a, _ in steps)

    def at(s):
        for a, step in steps:
            if 0 <= s + a < total:
                step(s + a, (s + a) % slots, (s + a) // slots)

    loops = (total - ahead - peel) // slots - 1
    for s in range(-ahead, slots):
        at(s)
    with eng.Fori(0, loops) as i:
        if chain:
            chain.loop(i, sum(counts) * slots)
        for u in range(slots, 2 * slots):
            for a, step in steps:
                step(i * slots + (u + a), (u + a) % slots, i + (u + a) // slots)
        if chain:
            chain.end(loops)
    for s in range((loops + 1) * slots, total):
        at(s)


def settle(eng, m):
    eng.sem_inc(m.settled, 1)


def row_broadcast(v, rows, cols):
    return bass.AP(tensor=v.tensor, offset=v.offset, ap=[[0, rows], [1, cols]])


def program(nc, x, src, dst, typ, thetas, phis, gammas, betas, rel, msg_w, msg_b, upd_w, upd_b, gate_w, gate_b, out):
    ctx = ExitStack()
    with ctx:
        def sb(name, shape, dt):
            return ctx.enter_context(nc.sbuf_tensor(name, shape, dt))

        def dram(name, shape, dt):
            return nc.dram_tensor(name, shape, dt, kind="Internal").ap()

        m = Program()
        m.x, m.src, m.dst, m.typ, m.thetas, m.phis, m.gammas, m.betas = x, src, dst, typ, thetas, phis, gammas, betas
        m.rel, m.msg_w, m.msg_b, m.upd_w, m.upd_b, m.gate_w, m.gate_b, m.out = rel, msg_w, msg_b, upd_w, upd_b, gate_w, gate_b, out
        m.node_table = dram("node_table", (2 * P * LO, 2), I32)
        m.rel_table = dram("rel_table", (R, D + 1), F32)
        m.keys = dram("keys", (EP,), I32)
        m.sorted = dram("sorted_edges", (EP, SW), F32)
        m.settled = ctx.enter_context(nc.semaphore("settled"))
        m.go = ctx.enter_context(nc.semaphore("go"))
        m.projected = dram("projected", (EP + P, D), F32)
        m.rewritten = dram("rewritten", (EP, D), F32)
        m.messages = dram("messages", (EP, D), F32)
        m.dkeys = dram("dkeys", (EP,), I32)
        m.ident = sb("ident", [P, P], F32)
        m.identb = sb("identb", [P, P], BF16)
        m.ones = sb("ones", [P, P], F32)
        m.before = sb("before", [P, P], F32)
        m.iota = sb("iota", [P, LO], BF16)
        m.earlier = sb("earlier", [P, 2, CW], BF16)
        m.eps = sb("eps", [P, 1], F32)
        m.zerob = sb("zerob", [P, LO], BF16)
        m.wt = sb("wt", [P, L, 2, 2, D], F32)
        m.upd = sb("upd", [P, 2, D], F32)
        m.msg = sb("msg", [P, 2, D], F32)
        m.updb = sb("updb", [P, D], F32)
        m.msgb = sb("msgb", [P, D], F32)
        m.gam = sb("gam", [P, L, 2], F32)
        m.bet = sb("bet", [P, L, 2], F32)
        m.srcf = sb("srcf", [P, TILES], F32)
        m.dstf = sb("dstf", [P, TILES], F32)
        m.hl = sb("hl", [P, 4, TILES], F32)
        m.gidx = sb("gidx", [P, 3, TILES], I32)
        m.ranks = sb("ranks", [P, TILES], I32)
        m.last_src = sb("last_src", [P, TILES], I32)
        m.big = sb("big", [P, 2 * (EP + 2)], F32)
        m.same = sb("same", [P, EP + 1], BF16)
        m.base = sb("base", [P, 2, 2, LO], BF16)
        m.cnt = sb("cnt", [P, 2, 2, LO], BF16)
        m.psum = ctx.enter_context(nc.psum_tensor("banks", [P, 8, 512], F32))
        m.feat = m.big[:, :].rearrange("p (h k) -> p h k", h=2)
        m.meta = sb("meta", [P, TILES, SW - C_S], F32)
        m.sums = sb("sums", [P, 2, 2, CHUNKS], F32)
        m.coef = sb("coef", [P, 3, 2], F32)

        def run(stage, *layer):
            m.stage += 1
            sems = []

            def stage_sem(name):
                sems.append(nc.alloc_semaphore(name=f"{name}_{m.stage}"))
                return sems[-1]

            m.sem = stage_sem
            with ExitStack() as own:
                m.sb = lambda name, shape, dt: own.enter_context(nc.sbuf_tensor(f"{name}_{m.stage}", shape, dt))
                stage(nc, m, *layer)
            nc.clear_and_free_semaphores(sems)
            nc.all_engine_barrier()

        m.stage = -1
        run(setup)
        run(count_nodes)
        run(rank_and_layer0)
        run(scan_forward, 0)
        for l in range(1, L):
            run(project, l)
            run(scan_forward, l)
        run(messages)
        run(all_nodes)
        run(rewrite_sources)
        run(add_messages)


def setup(nc, m):
    sb, sem, ps = m.sb, m.sem, m.psum
    ids = sb("ids", [TILES, 3, P], I32)
    idf = sb("idf", [TILES, 3, P], F32)
    raw = m.big[:, 0:2 * 2 * L * D].rearrange("p (w l h k) -> p w l h k", w=2, l=L, h=2)
    cliff = m.big[:, 3072:3072 + 2 * 2 * D].rearrange("p (w h k) -> p w h k", w=2, h=2)
    relr = m.big[:, 4096:4096 + 4 * (D + 1)].rearrange("p (t k) -> p t k", t=4)
    rowb = m.big[:, 5200:5200 + 4 * D].rearrange("p (w k) -> p w k", w=4)
    bcol = m.big[:, 6300:6302]
    bcols = m.big[:, 6400:6400 + 2 * P].rearrange("p (h k) -> p h k", h=2)
    gz = m.big[:, 6700:6708]
    zrow = m.big[:, 7500:7500 + D]
    iotai = m.big[:, 7000:7000 + LO].bitcast(I32)
    idi = m.big[:, 8000:8000 + 6 * TILES].bitcast(I32).rearrange("p (w t) -> p w t", w=6)
    idc = m.big[:, 9000:9000 + 4 * TILES].rearrange("p (w t) -> p w t", w=4)
    init, ids_in, keys_out, w_in, c_in, b_in, r_in = (sem(n) for n in ("init", "ids_in", "keys_out", "w_in", "c_in", "b_in", "r_in"))
    consts, idf_ready, id_ps, wd_ready, w_ps, w_used, cl_ready, cl_ps = (
        sem(n) for n in ("consts", "idf_ready", "id_ps", "wd_ready", "w_ps", "w_used", "cl_ready", "cl_ps"))
    kup_ready, msg_ps, gate_z, gate_s, rel_out, bc_ready = (sem(n) for n in ("kup_ready", "msg_ps", "gate_z", "gate_s", "rel_out", "bc_ready"))
    dump_out = sem("dump_out")
    dve_own, pool_own = sem("dve_own0"), sem("pool_own0")
    NEG = {(0, 3), (1, 2), (2, 3)}
    BLOCK = [[0, 1, 2, 3], [1, 0, 3, 2], [2, 3, 0, 1], [3, 2, 1, 0]]

    with nc.Block() as block:
        @block.gpsimd
        def _(g):
            chain = Chain(g, pool_own)
            g.memset(ids[:, 0:2, :], PAD_KEY)
            g.memset(ids[:, 2:3, :], 0).then_inc(init, 1)
            g.memset(m.ident[:, :], 0.0)
            g.memset(m.ones[:, :], 1.0)
            g.memset(m.earlier[:, :, :], 1.0)
            g.memset(m.zerob[:, :], 0.0)
            chain(g.memset(m.eps[:, :], EPS))
            g.affine_select(out=m.ident[:, :], in_=m.ident[:, :], compare_op=ALU.not_equal, fill=1.0,
                            base=0, pattern=[[-1, P]], channel_multiplier=1)
            g.affine_select(out=m.before[:, :], in_=m.ones[:, :], compare_op=ALU.is_gt, fill=0.0,
                            base=0, pattern=[[1, P]], channel_multiplier=-1)
            g.affine_select(out=m.earlier[:, :, :], in_=m.earlier[:, :, :], compare_op=ALU.is_gt, fill=0.0,
                            base=0, pattern=[[P, 2], [-1, CW]], channel_multiplier=1)
            g.iota(iotai, pattern=[[1, LO]], base=0, channel_multiplier=0).then_inc(consts, 1)
            g.memset(zrow, 0.0).then_inc(m.go, 1)

        @block.sync
        def _(sp):
            sp.wait_ge(init, 1)
            for w, v in enumerate((m.src, m.dst, m.typ)):
                sp.dma_start(ids[0:LAST, w, :], v[0:LAST * P].rearrange("(t p) -> t p", p=P)).then_inc(ids_in, 16)
                sp.dma_start(ids[LAST:LAST + 1, w, 0:LASTN],
                             v[LAST * P:E].rearrange("(a p) -> a p", a=1)).then_inc(ids_in, 16)
            sp.wait_ge(ids_in, 6 * 16)
            sp.dma_start(m.keys.rearrange("(t p) -> t p", p=P), ids[:, 0, :]).then_inc(keys_out, 16)
            sp.dma_start(m.dkeys.rearrange("(t p) -> t p", p=P), ids[:, 1, :]).then_inc(keys_out, 16)
            for l in range(L):
                for w, v in enumerate((m.thetas, m.phis)):
                    sp.dma_start(raw[:, w, l, :, :], v[l].rearrange("(h p) k -> p h k", p=P)).then_inc(w_in, 16)
            for w, v in enumerate((m.msg_w, m.upd_w)):
                for a in range(4):
                    for b in range(4):
                        sp.dma_start(cliff[64 * (a % 2):64 * (a % 2) + 64, w, a // 2, 64 * b:64 * b + 64],
                                     v[BLOCK[a][b]]).then_inc(c_in, 16)
            sp.dma_start(relr[0:RT, :, 0:D], m.rel.rearrange("(t p) k -> p t k", p=RT)).then_inc(r_in, 16)
            sp.dma_start(rowb[:, 0, :], row_broadcast(m.gate_w[0], P, D)).then_inc(b_in, 16)
            sp.dma_start(rowb[:, 2, :], row_broadcast(m.upd_b.rearrange("a b -> (a b)"), P, D)).then_inc(b_in, 16)
            sp.dma_start(gz[:, 0:1], row_broadcast(m.gate_b, P, 1)).then_inc(b_in, 16)
            for h in range(2):
                sp.dma_start(bcol[:, h:h + 1], m.msg_b.rearrange("(h a) b -> h (a b)", h=2)[h].rearrange("(p o) -> p o", o=1)).then_inc(b_in, 16)
                for l in range(L):
                    sp.dma_start(m.gam[:, l, h:h + 1], m.gammas[l, h * P:(h + 1) * P].rearrange("(p o) -> p o", o=1)).then_inc(b_in, 16)
                    sp.dma_start(m.bet[:, l, h:h + 1], m.betas[l, h * P:(h + 1) * P].rearrange("(p o) -> p o", o=1)).then_inc(b_in, 16)
            sp.wait_ge(m.go, 1)
            sp.dma_start(m.out[N:N + P, :], zrow).then_inc(dump_out, 16)
            sp.wait_ge(gate_s, 1)
            sp.dma_start(m.rel_table.rearrange("(t p) k -> p t k", p=RT), relr[0:RT, :, :]).then_inc(rel_out, 16)
            sp.wait_ge(rel_out, 16)
            sp.wait_ge(dump_out, 16)
            sp.wait_ge(keys_out, 32)

        @block.vector
        def _(v):
            chain = Chain(v, dve_own)
            v.wait_ge(consts, 1)
            v.tensor_copy(m.identb[:, :], m.ident[:, :])
            v.tensor_copy(m.iota[:, :], iotai)
            v.wait_ge(ids_in, 6 * 16)
            v.tensor_copy(idf[:, :, :], ids[:, :, :]).then_inc(idf_ready, 1)
            v.wait_ge(id_ps, 1)
            pid = ps[:, 0, 0:3 * P].rearrange("p (w t) -> p w t", w=3)[:, :, 0:TILES]
            v.tensor_copy(m.srcf[:, :], pid[:, 0, :])
            v.tensor_copy(m.dstf[:, :], pid[:, 1, :])
            v.tensor_copy(idc[:, 0:3, :], pid)
            chain(v.tensor_copy(idi[:, 0:3, :], pid))
            for w in range(2):
                v.tensor_scalar(idi[:, 3 + w, :], idi[:, w, :], 8, None, ALU.arith_shift_right)
                chain(v.tensor_scalar(idi[:, w, :], idi[:, w, :], LO - 1, None, ALU.bitwise_and))
                v.tensor_copy(m.hl[:, 2 * w, :], idi[:, 3 + w, :])
                v.tensor_copy(m.hl[:, 2 * w + 1, :], idi[:, w, :])
                v.scalar_tensor_tensor(m.gidx[:, w, :], idc[:, w, :], float(N), idc[:, w, :], ALU.is_lt, ALU.mult)
            v.tensor_copy(m.gidx[:, 2, :], idc[:, 2, :])
            v.wait_ge(w_in, 6 * 16)
            for l in range(L):
                v.tensor_sub(raw[:, 1, l, :, :], raw[:, 1, l, :, :], raw[:, 0, l, :, :]).then_inc(wd_ready, 1)
            v.wait_ge(c_in, 32 * 16)
            for a, b in sorted(NEG):
                s = 64 * (a % 2)
                blk = cliff[s:s + 64, :, a // 2, 64 * b:64 * b + 64]
                last = v.tensor_scalar(blk, blk, -1.0, None, ALU.mult)
            last.then_inc(cl_ready, 1)
            for n in range(2 * L):
                v.wait_ge(w_ps, n + 1)
                l, w = n // 2, n % 2
                v.tensor_copy(m.wt[:, l, w, :, :], ps[:, 2 + n % 2, :].rearrange("p (h k) -> p h k", h=2)).then_inc(w_used, 1)
            v.wait_ge(cl_ps, 1)
            v.tensor_copy(m.upd[:, :, :].rearrange("p h (c b) -> p h b c", b=4),
                          ps[:, 4, :].rearrange("p (h b c) -> p h b c", h=2, b=4)).then_inc(kup_ready, 1)
            v.wait_ge(b_in, 17 * 16)
            v.tensor_copy(m.updb[:, :].rearrange("p (c b) -> p b c", b=4), rowb[:, 2, :].rearrange("p (b c) -> p b c", b=4))
            v.tensor_copy(rowb[:, 1, :].rearrange("p (b c) -> p b c", b=4), rowb[:, 0, :].rearrange("p (c b) -> p b c", b=4))
            for h in range(2):
                last = v.tensor_scalar(bcols[:, h, :], m.ones[:, :], bcol[:, h:h + 1], None, ALU.mult)
            last.then_inc(bc_ready, 1)
            v.wait_ge(bc_ready, 1)
            v.wait_ge(r_in, 16)
            for t in range(4):
                chain(v.scalar_tensor_tensor(rowb[0:RT, 3, :], relr[0:RT, t, 0:D], 1.0, rowb[0:RT, 1, :], ALU.mult, ALU.mult,
                                             accum_out=gz[0:RT, 1 + t:2 + t]))
            v.engine_nop().then_inc(gate_z, 1)
            v.wait_ge(msg_ps, 1)
            v.tensor_copy(m.msg[:, :, :], ps[:, 5, :].rearrange("p (h k) -> p h k", h=2))
            chain(v.tensor_copy(m.msgb[:, :], ps[:, 6, 0:D]))

        @block.scalar
        def _(a):
            a.wait_ge(gate_z, 1)
            a.activation(relr[0:RT, :, D], gz[0:RT, 1:5], ACT.Sigmoid, bias=gz[0:RT, 0:1]).then_inc(gate_s, 1)

        @block.tensor
        def _(pe):
            pe.wait_ge(idf_ready, 1)
            for w in range(3):
                last = pe.transpose(ps[:, 0, w * P:w * P + TILES], idf[:, w, :], m.ident[0:TILES, 0:TILES])
            last.then_inc(id_ps, 1)
            pe.wait_ge(wd_ready, L)
            for n in range(2 * L):
                l, w = n // 2, n % 2
                if n >= 2:
                    pe.wait_ge(w_used, n - 1)
                for kh in range(2):
                    for oh in range(2):
                        last = pe.transpose(ps[:, 2 + n % 2, kh * D + oh * P:kh * D + oh * P + P],
                                            raw[:, w, l, oh, kh * P:kh * P + P], m.ident[:, :])
                last.then_inc(w_ps, 1)
            pe.wait_ge(cl_ready, 1)
            for kh in range(2):
                for oh in range(2):
                    last = pe.transpose(ps[:, 4, kh * D + oh * P:kh * D + oh * P + P],
                                        cliff[:, 1, oh, kh * P:kh * P + P], m.ident[:, :])
            last.then_inc(cl_ps, 1)
            pe.wait_ge(kup_ready, 1)
            pe.wait_ge(bc_ready, 1)
            for kh in range(2):
                for mh in range(2):
                    pe.matmul(ps[:, 5, kh * D:kh * D + D], cliff[:, 0, mh, kh * P:kh * P + P], m.upd[:, mh, :],
                              start=(mh == 0), stop=(mh == 1))
            for mh in range(2):
                last = pe.matmul(ps[:, 6, 0:D], bcols[:, mh, :], m.upd[:, mh, :], start=(mh == 0), stop=(mh == 1))
            last.then_inc(msg_ps, 1)


def count_nodes(nc, m):
    sb, sem, ps = m.sb, m.sem, m.psum
    m.hot = m.big[:, 0:TILES * 2 * LO // 2].bitcast(BF16).rearrange("p (t w k) -> p t w k", t=TILES, w=2)
    hotd = sb("hotd", [P, 2, 2, LO], BF16)
    cntf = sb("cntf", [P, 2, 2, LO], F32)
    incl = sb("incl", [P, 2, LO], F32)
    basef = sb("basef", [P, 2, LO], F32)
    off = sb("off", [P, 2], F32)
    tmp = sb("tmp1", [P, 2, LO], F32)
    table = sb("table", [P, 2, LO, 2], I32)
    hots_ready, hots_used, cnt_ps, tot_ready, off_ps, table_ready, table_out = (
        sem(n) for n in ("hots_ready", "hots_used", "cnt_ps", "tot_ready", "off_ps", "table_ready", "table_out"))
    dve_own = sem("dve_own1")

    with nc.Block() as block:
        @block.vector
        def _(v):
            def hots(t, slot):
                v.tensor_scalar(m.hot[:, bass.ds(t, 1), 0, :].rearrange("p a k -> p (a k)"), m.iota[:, :], m.hl[:, 0, bass.ds(t, 1)], None, ALU.is_equal)
                v.tensor_scalar(m.hot[:, bass.ds(t, 1), 1, :].rearrange("p a k -> p (a k)"), m.iota[:, :], m.hl[:, 1, bass.ds(t, 1)], None, ALU.is_equal)
                v.wait_ge(hots_used, t + 1)
                v.tensor_scalar(hotd[:, slot, 0, :], m.iota[:, :], m.hl[:, 2, bass.ds(t, 1)], None, ALU.is_equal)
                v.tensor_scalar(hotd[:, slot, 1, :], m.iota[:, :], m.hl[:, 3, bass.ds(t, 1)], None,
                                ALU.is_equal).then_inc(hots_ready, 1)

            with v.Fori(0, TILES // 2) as i:
                for slot in range(2):
                    hots(i * 2 + slot, slot)
            chain = Chain(v, dve_own)
            v.wait_ge(cnt_ps, 1)
            chain(v.tensor_copy(cntf[:, :, :, :], ps[:, 0:4, 0:LO].rearrange("p (w h) k -> p w h k", w=2)))
            chain(v.tensor_copy(m.cnt[:, 0, :, :], cntf[:, 0, :, :]))
            v.tensor_sub(m.cnt[:, 1, :, :], cntf[:, 0, :, :], m.cnt[:, 0, :, :])
            v.memset(basef[:, :, :], 0.0)
            v.memset(tmp[:, :, :], 1.0).then_inc(dve_own, 1)
            chain.k += 1
            v.wait_ge(dve_own, chain.k)
            for h in range(2):
                last = v.tensor_tensor_scan(incl[:, h, :], tmp[:, h, :], cntf[:, 0, h, :], 0.0, ALU.mult, ALU.add)
            last.then_inc(tot_ready, 1)
            v.wait_ge(off_ps, 1)
            chain(v.tensor_copy(off[:, :], ps[:, 4, 0:2]))
            for h in range(2):
                last = v.scalar_tensor_tensor(basef[:, h, :], incl[:, h, :], off[:, h:h + 1], cntf[:, 0, h, :], ALU.add, ALU.subtract)
            chain(last)
            chain(v.tensor_copy(m.base[:, 0, :, :], basef[:, :, :]))
            v.tensor_sub(m.base[:, 1, :, :], basef[:, :, :], m.base[:, 0, :, :])
            chain(v.scalar_tensor_tensor(tmp[:, :, :], basef[:, :, :], -1.0 - CROW, cntf[:, 0, :, :], ALU.add, ALU.add))
            chain(v.scalar_tensor_tensor(tmp[:, :, :], cntf[:, 0, :, :], 0.0, tmp[:, :, :], ALU.is_gt, ALU.mult))
            v.tensor_scalar(table[:, :, :, 0], tmp[:, :, :], float(CROW), None, ALU.add)
            v.tensor_copy(table[:, :, :, 1].bitcast(F32), cntf[:, 1, :, :]).then_inc(table_ready, 1)

        @block.tensor
        def _(pe):
            pe.sem_inc(hots_used, 2)

            def count(t, slot, start, stop):
                pe.wait_ge(hots_ready, t + 1)
                hot = m.hot[:, bass.ds(t, 1), :, :].rearrange("p a w k -> p (a w) k")
                for h in range(2):
                    pe.matmul(ps[:, h, 0:LO], hot[:, 0, h * P:h * P + P], hot[:, 1, :], start=start, stop=stop)
                for h in range(2):
                    last = pe.matmul(ps[:, 2 + h, 0:LO], hotd[:, slot, 0, h * P:h * P + P], hotd[:, slot, 1, :], start=start, stop=stop)
                last.then_inc(hots_used, 1)
                return last

            count(0, 0, True, False)
            count(1, 1, False, False)
            with pe.Fori(1, TILES // 2 - 1) as i:
                for slot in range(2):
                    count(i * 2 + slot, slot, False, False)
            count(TILES - 2, 0, False, False)
            count(TILES - 1, 1, False, True)
            pe.matmul(ps[:, 5, 0:1], m.ones[:, :], m.ones[:, 0:1], start=True, stop=True).then_inc(cnt_ps, 1)
            pe.wait_ge(tot_ready, 1)
            pe.matmul(ps[:, 4, 0:2], m.before[:, :], incl[:, :, LO - 1], start=True, stop=False)
            pe.matmul(ps[:, 4, 1:2], m.ones[:, :], incl[:, 0, LO - 1:LO], start=False, stop=True).then_inc(off_ps, 1)

        @block.sync
        def _(sp):
            sp.wait_ge(table_ready, 1)
            for h in range(2):
                sp.dma_start(m.node_table.rearrange("(h p k) w -> h p (k w)", h=2, p=P)[h],
                             table[:, h, :, :].rearrange("p k w -> p (k w)")).then_inc(table_out, 16)
            sp.wait_ge(table_out, 32)


def rank_and_layer0(nc, m):
    sb, sem, ps = m.sb, m.sem, m.psum
    SLOTS = 4
    TS = 2 * SLOTS
    row = [sb(f"row{j}", [P, SW], F32) for j in range(TS)]
    xd = [sb(f"xd{j}", [P, D], F32) for j in range(TS)]
    nt = [sb(f"nt{j}", [P, 2], I32) for j in range(TS)]
    gi = [sb(f"gi{j}", [P, 3], I32) for j in range(TS)]
    place = [sb(f"place{j}", [P, 1], I32) for j in range(TS)]
    stats = sb("stats", [P, 4, 6], F32)
    mv = sb("mv", [P, 4, 2], F32)
    std = sb("std", [P, 4], F32)
    rstd = sb("rstd", [P, 4], F32)
    nmr = sb("nmr", [P, 4], F32)
    h = sb("h", [P, 4, D], F32)
    hT = sb("hT", [P, 4, CW], F32)
    hotT = sb("hotT", [P, 4, P], BF16)
    run = sb("run", [P, 2, 2, LO], BF16)
    junk = m.meta[:, :, :].rearrange("p t w -> p (t w)")[:, 0:3 * CW].bitcast(BF16).rearrange("p (n k) -> p n k", n=6)
    keys = sb("keys_of_chunk", [P, 2, CW], I32)
    occ = sb("occ", [P, 2, 2], F32)
    looked = sb("looked", [P, 2], F32)
    rankf = sb("rankf", [P, 2], F32)
    degs = sb("degs", [P, 2], F32)
    prod = sb("prod", [P, 2], F32)
    root = sb("root", [P, 2], F32)
    gathered = [sem(f"gathered{q}") for q in range(SLOTS)]
    scattered = [sem(f"scattered{q}") for q in range(SLOTS)]
    keys_in = [sem(f"keys_in{q}") for q in range(SLOTS)]
    (idx_ready, mv_ready, std_ready, ln_ready, h_ready, hT_ps, hT_ready, e_ready, hotT_ps, hotT_ready, looked_up,
     sel_done, run_ps, run_ready, prod_ready, root_ready, row_ready, dve_own) = (sem(n) for n in (
         "idx_ready", "mv_ready", "std_ready", "ln_ready", "h_ready", "hT_ps", "hT_ready", "e_ready", "hotT_ps",
         "hotT_ready", "looked_up", "sel_done", "run_ps", "run_ready", "prod_ready", "root_ready", "row_ready", "dve_own2"))
    occ_done = Signal(sem("occ_done"), 1)

    with nc.Block() as block:
        @block.sync
        def _(sp):
            def load_keys(c, q, turn):
                sp.wait_ge(occ_done.sem, occ_done.free(c, 2))
                sp.dma_start(keys[:, q % 2, :], bass.AP(tensor=m.keys.tensor, offset=c * CW, ap=[[0, P], [1, CW]]))\
                  .then_inc(keys_in[q], 16)

            staged(sp, CHUNKS, SLOTS, (0, load_keys))

        @block.gpsimd
        def _(g):
            for j in range(TS):
                g.memset(row[j][:, C_KEY:SW], 0.0)

            def gather(c, q, turn):
                g.wait_ge(scattered[q], turn * 32)
                for u in range(2):
                    last = g.tensor_copy(gi[2 * q + u][:, :], m.gidx[:, :, bass.ds(c * 2 + u, 1)].rearrange("p w a -> p (w a)"))
                last.then_inc(idx_ready, 1)
                g.wait_ge(idx_ready, c + 1)
                settle(g, m)
                for j in (2 * q, 2 * q + 1):
                    for to, table, w in ((xd[j][:, :], m.x, 1), (row[j][:, C_X:C_X + D], m.x, 0),
                                         (row[j][:, C_R:C_S + 1], m.rel_table, 2), (nt[j][:, :], m.node_table, 1)):
                        g.indirect_dma_start(out=to, out_offset=None, in_=table,
                                             in_offset=bass.IndirectOffsetOnAxis(ap=gi[j][:, w:w + 1], axis=0)).then_inc(gathered[q], 16)

            def scatter(c, q, turn):
                g.wait_ge(row_ready, c * 2 + 2)
                settle(g, m)
                for j in (2 * q, 2 * q + 1):
                    g.indirect_dma_start(out=m.sorted, out_offset=bass.IndirectOffsetOnAxis(ap=place[j][:, 0:1], axis=0),
                                         in_=row[j][:, :], in_offset=None).then_inc(scattered[q], 16)

            staged(g, CHUNKS, SLOTS, (0, scatter), (3, gather))
            for q in range(SLOTS):
                g.wait_ge(scattered[q], len(range(q, CHUNKS, SLOTS)) * 32)

        @block.vector
        def _(v):
            chain = Chain(v, dve_own)
            v.sem_inc(occ_done.sem, occ_done.ahead)
            v.memset(run[:, :, :, :], 0.0).then_inc(run_ready, 1)

            def statistics(c, q, turn):
                slots = (2 * q, 2 * q + 1)
                v.wait_ge(gathered[q], (turn + 1) * 8 * 16)
                for u, j in enumerate(slots):
                    v.bn_stats(stats[:, u, :], xd[j][:, :])
                    last = v.bn_stats(stats[:, 2 + u, :], row[j][:, C_X:C_X + D])
                chain(last)
                settle(v, m)
                for n in range(4):
                    last = v.bn_aggr(mv[:, n, :], stats[:, n, :])
                last.then_inc(mv_ready, 1)

            def scales(c, q, turn):
                v.wait_ge(std_ready, c + 1)
                v.wait_ge(h_ready, c)
                chain(v.reciprocal(rstd[:, :], std[:, :]))
                v.scalar_tensor_tensor(nmr[:, :], mv[:, :, 0], -1.0, rstd[:, :], ALU.mult, ALU.mult).then_inc(ln_ready, 1)

            def count_equal(c, q, turn):
                v.wait_ge(keys_in[q], (turn + 1) * 16)
                for u in range(2):
                    last = v.scalar_tensor_tensor(junk[:, u, :], keys[:, q % 2, :], m.srcf[:, bass.ds(c * 2 + u, 1)],
                                                  m.earlier[:, u, :], ALU.is_equal, ALU.mult, accum_out=occ[:, 0, u:u + 1])
                last.then_inc(occ_done.sem, 1)

            def place_edges(c, q, turn):
                slots = (2 * q, 2 * q + 1)
                v.wait_ge(looked_up, c + 1)
                for u in range(2):
                    hot = m.hot[:, bass.ds(c * 2 + u, 1), 1, :].rearrange("p a k -> p (a k)")
                    v.scalar_tensor_tensor(junk[:, 2 + u, :], ps[:, 4, u * LO:u * LO + LO], 1.0, hot, ALU.mult, ALU.mult,
                                           accum_out=looked[:, u:u + 1])
                    last = v.scalar_tensor_tensor(junk[:, 4 + u, :], ps[:, 5, u * LO:u * LO + LO], 1.0, hot, ALU.mult, ALU.mult,
                                                  accum_out=degs[:, u:u + 1])
                last.then_inc(sel_done, 1)
                v.wait_ge(sel_done, c + 1)
                v.wait_ge(occ_done.sem, occ_done.done(c))
                v.tensor_tensor(rankf[:, :], looked[:, :], occ[:, 0, :], ALU.add)
                for u, j in enumerate(slots):
                    last = v.tensor_tensor(prod[:, u:u + 1], degs[:, u:u + 1], nt[j][:, 1:2].bitcast(F32), ALU.mult)
                chain(last)
                chain(v.tensor_scalar(prod[:, :], prod[:, :], 1.0, None, ALU.max))
                v.tensor_copy(m.ranks[:, bass.ds(c * 2, 2)], rankf[:, :]).then_inc(prod_ready, 1)
                for u, j in enumerate(slots):
                    v.tensor_copy(place[j][:, :], rankf[:, u:u + 1])
                    v.tensor_copy(row[j][:, C_POS:C_POS + 1].bitcast(I32), nt[j][:, 0:1])
                    v.tensor_copy(row[j][:, C_KEY:C_KEY + 1], m.srcf[:, bass.ds(c * 2 + u, 1)])

            def keep_counts(c, q, turn):
                v.wait_ge(run_ps, c + 1)
                chain(v.tensor_copy(run[:, 0, :, :], ps[:, 6:8, 0:LO]))
                v.tensor_sub(run[:, 1, :, :], ps[:, 6:8, 0:LO], run[:, 0, :, :]).then_inc(run_ready, 1)

            def scale_of_edge(c, q, turn):
                v.wait_ge(root_ready, c + 1)
                chain(v.reciprocal(root[:, :], root[:, :]))
                for u in range(2):
                    s = row[2 * q + u][:, C_S:C_S + 1]
                    last = v.tensor_tensor(s, s, root[:, u:u + 1], ALU.mult)
                chain(last)

            def finish(c, q, turn):
                v.wait_ge(e_ready, c + 1)
                for u in range(2):
                    v.tensor_scalar(row[2 * q + u][:, C_E:C_E + D], ps[:, 2, u * D:u * D + D], 0.0, None, ALU.max).then_inc(row_ready, 1)

            staged(v, CHUNKS, SLOTS, (0, finish), (2, statistics), (2, scales), (1, count_equal), (1, place_edges),
                   (1, keep_counts), (1, scale_of_edge), chain=chain, counts=(0, 1, 1, 0, 2, 1, 2))

        @block.scalar
        def _(a):
            def one_hots(c, q, turn):
                a.wait_ge(hotT_ps, c + 1)
                a.wait_ge(looked_up, c)
                a.activation(hotT[:, :, :].rearrange("p a k -> p (a k)"), ps[:, 3, :], ACT.Copy).then_inc(hotT_ready, 1)

            def normalise(c, q, turn):
                a.wait_ge(ln_ready, c + 1)
                a.wait_ge(hT_ps, c)
                for u in range(2):
                    j = 2 * q + u
                    a.activation(h[:, u, :], xd[j][:, :], ACT.Relu, bias=nmr[:, u:u + 1], scale=rstd[:, u:u + 1])
                    last = a.activation(h[:, 2 + u, :], row[j][:, C_X:C_X + D], ACT.Relu,
                                        bias=nmr[:, 2 + u:3 + u], scale=rstd[:, 2 + u:3 + u])
                last.then_inc(h_ready, 1)

            def root_of_degrees(c, q, turn):
                a.wait_ge(prod_ready, c + 1)
                a.activation(root[:, :], prod[:, :], ACT.Sqrt).then_inc(root_ready, 1)

            def transposed(c, q, turn):
                a.wait_ge(hT_ps, c + 1)
                a.wait_ge(e_ready, c)
                for s in range(2):
                    last = a.activation(hT[:, 2 * s:2 * s + 2, :].rearrange("p a k -> p (a k)"), ps[:, s, :], ACT.Copy)
                last.then_inc(hT_ready, 1)

            def root_of_variance(c, q, turn):
                a.wait_ge(mv_ready, c + 1)
                a.activation(std[:, :], mv[:, :, 1], ACT.Sqrt, bias=m.eps[:, :]).then_inc(std_ready, 1)

            staged(a, CHUNKS, SLOTS, (2, root_of_variance), (1, transposed), (2, normalise), (2, one_hots), (1, root_of_degrees))

        @block.tensor
        def _(pe):
            for hh in range(2):
                pe.matmul(ps[:, 6 + hh, 0:LO], m.zerob[:, 0:P], m.zerob[:, :], start=True, stop=True)

            def turn_one_hots(c, q, turn):
                hot = m.hot[:, bass.ds(c * 2, 2), :, :]
                for n in range(4):
                    last = pe.matmul(ps[:, 3, n * P:n * P + P], hot[:, n // 2, 0, (n % 2) * P:(n % 2) * P + P],
                                     m.identb[:, :], start=True, stop=True)
                last.then_inc(hotT_ps, 1)

            def rank(c, q, turn):
                hot = m.hot[:, bass.ds(c * 2, 2), :, :]
                pe.wait_ge(hotT_ready, c + 1)
                pe.wait_ge(run_ready, c + 1)
                pe.wait_ge(sel_done, c)
                for u in range(2):
                    for n in range(8):
                        table = (m.base, run)[n // 4]
                        pe.matmul(ps[:, 4, u * LO:u * LO + LO], hotT[:, 2 * u + n % 2, :], table[:, n // 2 % 2, n % 2, :],
                                  start=(n == 0), stop=(n == 7))
                    for n in range(4):
                        last = pe.matmul(ps[:, 5, u * LO:u * LO + LO], hotT[:, 2 * u + n % 2, :], m.cnt[:, n // 2, n % 2, :],
                                         start=(n == 0), stop=(n == 3))
                last.then_inc(looked_up, 1)
                for n in range(4):
                    u, hh = n // 2, n % 2
                    last = pe.matmul(ps[:, 6 + hh, 0:LO], hot[:, u, 0, hh * P:hh * P + P], hot[:, u, 1, :], start=False, stop=True,
                                     skip_group_check=True)
                last.then_inc(run_ps, 1)

            def turn_features(c, q, turn):
                pe.wait_ge(h_ready, c + 1)
                for n in range(8):
                    side, u, kh = n // 4, n // 2 % 2, n % 2
                    last = pe.transpose(ps[:, side, kh * CW + u * P:kh * CW + u * P + P],
                                        h[:, 2 * side + u, kh * P:kh * P + P], m.ident[:, :])
                last.then_inc(hT_ps, 1)

            def values(c, q, turn):
                pe.wait_ge(hT_ready, c + 1)
                pe.wait_ge(row_ready, c * 2)
                for u in range(2):
                    for n in range(4):
                        last = pe.matmul(ps[:, 2, u * D:u * D + D], hT[:, n, u * P:u * P + P], m.wt[:, 0, n // 2, n % 2, :],
                                         start=(n == 0), stop=(n == 3))
                last.then_inc(e_ready, 1)

            staged(pe, CHUNKS, SLOTS, (0, values), (1, turn_features), (1, rank), (2, turn_one_hots))


def scan_forward(nc, m, l):
    sb, ps = m.sb, m.psum
    sem = lambda n: m.sem(f"{n}_f{l}")
    SLOTS = 4
    rows = sb("rows", [P, 2 * SLOTS, D], F32)
    masked = sb("masked", [P, 2, 2, CW], F32)
    junk = sb("junk_f", [P, 2, 2, CW], BF16)
    t2 = sb("t2", [P, 8, 2], F32)
    loaded = [sem(f"loaded{q}") for q in range(SLOTS)]
    meta_in, diag_ready, pi_ready, dve_own = (sem(n) for n in ("meta_in", "diag_ready", "pi_ready", "dve_own"))
    masked_ready, var_ready, std_ready = (sem(n) for n in ("masked_ready", "var_ready", "std_ready"))
    val_ps = Signal(sem("val_ps"), SLOTS - 1)
    scanned = Signal(sem("scanned"), 1)
    squared = Signal(sem("squared"), 1)
    keys_ps, same_ready = Signal(sem("keys_ps"), 1), Signal(sem("same_ready"), 1)
    if l == 0:
        diag = sb("diag", [P, 2, 2, P], F32)
        krow = sb("krow", [P, 2, 1 + CW], F32)
    else:
        pidx = [sb(f"pidx{j}", [P, 1], I32) for j in range(2 * SLOTS)]

    with nc.Block() as block:
        @block.sync
        def _(sp):
            def load(c, q, turn):
                sp.wait_ge(val_ps.sem, val_ps.free(c, SLOTS))
                sp.dma_start(rows[:, 2 * q:2 * q + 2, :],
                             m.sorted[bass.ds(c * CW, CW), C_E:C_E + D].rearrange("(u p) k -> p u k", p=P)).then_inc(loaded[q], 16)

            if l == 0:
                sp.dma_start(m.meta[:, :, :], m.sorted.rearrange("(t p) w -> p t w", p=P)[:, :, C_S:SW]).then_inc(meta_in, 16)
                staged(sp, CHUNKS, SLOTS, (0, load))

        @block.gpsimd
        def _(g):
            def gather(c, q, turn):
                g.wait_ge(val_ps.sem, val_ps.free(c, SLOTS))
                for u in range(2):
                    last = g.tensor_copy(pidx[2 * q + u][:, :], m.meta[:, bass.ds(c * 2 + u, 1), 1].bitcast(I32))
                last.then_inc(pi_ready, 1)
                g.wait_ge(pi_ready, c + 1)
                settle(g, m)
                for j in (2 * q, 2 * q + 1):
                    g.indirect_dma_start(out=rows[:, j, :], out_offset=None, in_=m.projected,
                                         in_offset=bass.IndirectOffsetOnAxis(ap=pidx[j][:, :], axis=0)).then_inc(loaded[q], 16)

            if l > 0:
                staged(g, CHUNKS, SLOTS, (0, gather))

        @block.scalar
        def _(a):
            a.sem_inc(squared.sem, squared.ahead)

            def key_diagonals(c, q, turn):
                a.wait_ge(keys_ps.sem, keys_ps.free(c, 2))
                for u in range(2):
                    last = a.activation(diag[:, q % 2, u, :], m.ident[:, :], ACT.Copy, scale=m.meta[:, bass.ds(c * 2 + u, 1), 2])
                last.then_inc(diag_ready, 1)

            def squares(c, q, turn):
                a.wait_ge(masked_ready, c + 1)
                for h in range(2):
                    last = a.activation(junk[:, q % 2, h, :], masked[:, q % 2, h, :], ACT.Square,
                                        accum_out=m.sums[:, 1, h, bass.ds(c, 1)])
                last.then_inc(squared.sem, 1)

            if l == 0:
                a.wait_ge(meta_in, 16)
            if l == 0:
                staged(a, CHUNKS, SLOTS, (3, key_diagonals), (0, squares))
            else:
                staged(a, CHUNKS, SLOTS, (0, squares))
            a.wait_ge(var_ready, 1)
            a.activation(t2[:, 4, :], t2[:, 3, :], ACT.Sqrt, bias=m.eps[:, :]).then_inc(std_ready, 1)

        @block.tensor
        def _(pe):
            pe.sem_inc(val_ps.sem, val_ps.ahead)
            pe.sem_inc(keys_ps.sem, keys_ps.ahead)

            def key_rows(c, q, turn):
                pe.wait_ge(diag_ready, c + 1)
                pe.wait_ge(same_ready.sem, same_ready.free(c, 2))
                pe.matmul(ps[:, 4 + q % 2, 0:CW], m.ones[:, :], diag[:, q % 2, :, :].rearrange("p u k -> p (u k)"),
                          start=True, stop=True).then_inc(keys_ps.sem, 1)

            def values(c, q, turn):
                pe.wait_ge(loaded[q], (turn + 1) * (16 if l == 0 else 32))
                pe.wait_ge(scanned.sem, scanned.free(c, 2))
                for h in range(2):
                    o = ps[:, q % 2, h * CW:h * CW + CW]
                    for u in range(2):
                        data = rows[:, 2 * q + u, h * P:h * P + P]
                        if l == 0:
                            last = pe.transpose(o[:, u * P:u * P + P], data, m.ident[:, :])
                        else:
                            for kh in range(2):
                                pe.matmul(o[:, u * P:u * P + P], m.wt[:, l, 1, kh, h * P:h * P + P],
                                          m.feat[:, kh, bass.ds(c * CW + (1 + u * P), P)], start=(kh == 0), stop=False)
                            last = pe.matmul(o[:, u * P:u * P + P], data, m.ident[:, :], start=False, stop=True)
                last.then_inc(val_ps.sem, 1)

            if l == 0:
                staged(pe, CHUNKS, SLOTS, (2, key_rows), (0, values))
            else:
                staged(pe, CHUNKS, SLOTS, (0, values))

        @block.vector
        def _(v):
            chain = Chain(v, dve_own)
            v.sem_inc(scanned.sem, scanned.ahead)
            v.sem_inc(same_ready.sem, same_ready.ahead)
            if l == 0:
                v.memset(m.feat[:, :, 0:1], 0.0)
                v.memset(m.feat[:, :, EP + 1:EP + 2], 0.0)
                v.memset(m.same[:, EP:EP + 1], 0.0)
                chain(v.memset(krow[:, 1, CW:CW + 1], -1.0))

            def run_flags(c, q, turn):
                q = q % 2
                v.wait_ge(keys_ps.sem, keys_ps.done(c))
                v.tensor_copy(krow[:, q, 0:1], krow[:, 1 - q, CW:CW + 1])
                v.tensor_copy(krow[:, q, 1:1 + CW], ps[:, 4 + q, 0:CW]).then_inc(same_ready.sem, 1)
                v.wait_ge(same_ready.sem, same_ready.done(c))
                chain(v.tensor_tensor(m.same[:, bass.ds(c * CW, CW)], krow[:, q, 1:1 + CW], krow[:, q, 0:CW], ALU.is_equal))

            def scan(c, q, turn):
                same = m.same[:, bass.ds(c * CW, CW)]
                v.wait_ge(val_ps.sem, val_ps.done(c))
                for h in range(2):
                    last = v.tensor_tensor_scan(m.feat[:, h, bass.ds(c * CW + 1, CW)], same, ps[:, q % 2, h * CW:h * CW + CW],
                                                m.feat[:, h, bass.ds(c * CW, 1)], ALU.mult, ALU.max)
                last.then_inc(scanned.sem, 1)
                v.wait_ge(scanned.sem, scanned.done(c))
                v.wait_ge(squared.sem, squared.free(c, 2))
                for h in range(2):
                    last = v.scalar_tensor_tensor(masked[:, q % 2, h, :], same, 0.0, m.feat[:, h, bass.ds(c * CW, CW)],
                                                  ALU.is_equal, ALU.mult, accum_out=m.sums[:, 0, h, bass.ds(c, 1)])
                last.then_inc(masked_ready, 1)

            if l == 0:
                staged(v, CHUNKS, SLOTS, (1, run_flags), (0, scan), chain=chain, counts=(1, 0))
            else:
                staged(v, CHUNKS, SLOTS, (0, scan))
            v.wait_ge(masked_ready, CHUNKS)
            v.wait_ge(squared.sem, squared.done(CHUNKS - 1))
            chain(v.tensor_reduce(t2[:, 0:2, :].rearrange("p a b -> p (a b)"), m.sums[:, :, :, :].rearrange("p a h c -> p (a h) c"),
                                  mybir.AxisListType.X, ALU.add))
            chain(v.tensor_scalar(t2[:, 0:2, :], t2[:, 0:2, :], 1.0 / N, None, ALU.mult))
            chain(v.tensor_tensor(t2[:, 2, :], t2[:, 0, :], t2[:, 0, :], ALU.mult))
            v.tensor_tensor(t2[:, 3, :], t2[:, 1, :], t2[:, 2, :], ALU.subtract).then_inc(var_ready, 1)
            v.wait_ge(std_ready, 1)
            chain(v.reciprocal(t2[:, 5, :], t2[:, 4, :]))
            chain(v.tensor_tensor(m.coef[:, 0, :], t2[:, 5, :], m.gam[:, l, :], ALU.mult))
            chain(v.tensor_tensor(t2[:, 6, :], m.coef[:, 0, :], t2[:, 0, :], ALU.mult))
            chain(v.tensor_tensor(m.coef[:, 1, :], m.bet[:, l, :], t2[:, 6, :], ALU.subtract))
            chain(v.tensor_scalar(m.coef[:, 2, :], m.coef[:, 1, :], 0.0, None, ALU.max))


class BackwardScan:

    def __init__(self, nc, m, sem, used):
        self.m, self.used = m, used
        self.vals = m.sb("back_vals", [P, 2, 2, CW], F32)
        self.same = m.sb("back_same", [P, 2, CW], BF16)
        self.carry = m.sb("back_carry", [P, 2, 2, 1], F32)
        self.filled, self.done, self.start = sem("back_filled"), sem("back_done"), sem("back_start")

    def init(self, v):
        v.memset(self.carry[:, 1, :, :], 0.0).then_inc(self.start, 1)
        v.wait_ge(self.start, 1)

    def fill(self, v, j, q):
        v.wait_ge(self.used.sem, self.used.free(j, 2))
        settle(v, self.m)
        v.tensor_copy(self.same[:, q, :], self.m.same[:, bass.ds(from_end(j) * CW + 1, CW)])
        v.tensor_copy(self.vals[:, q, :, :], self.m.feat[:, :, bass.ds(from_end(j) * CW + 1, CW)]).then_inc(self.filled, 1)

    def scan(self, v, j, q):
        v.wait_ge(self.filled, j + 1)
        for h in range(2):
            f = self.vals[:, q, h, ::-1]
            last = v.tensor_tensor_scan(f, self.same[:, q, ::-1], f, self.carry[:, 1 - q, h, :], ALU.mult, ALU.max)
        last.then_inc(self.done, 1)
        v.wait_ge(self.done, j * 2 + 1)
        v.tensor_copy(self.carry[:, q, :, :], self.vals[:, q, :, 0:1]).then_inc(self.done, 1)
        v.wait_ge(self.done, j * 2 + 2)
        settle(v, self.m)

    def scanned(self, j):
        return j * 2 + 2


def from_end(j):
    return (CHUNKS - 1) - j


def project(nc, m, l):
    sb, ps = m.sb, m.psum
    sem = lambda n: m.sem(f"{n}_p{l}")
    xc = sb("xc_p", [P, 2, 2, CW], F32)
    crow = sb("crow", [P, 2, P], F32)
    rows = sb("rows_p", [P, 2, 2, D], F32)
    c_out = sb("c_out", [P, D], F32)
    c_ready, c_ps, cout_ready, cout_done = (sem(n) for n in ("c_ready", "c_ps", "cout_ready", "cout_done"))
    xc_ready, rows_ps, rows_ready, kept = (Signal(sem(n), 1) for n in ("xc_ready", "rows_ps", "rows_ready", "kept"))
    stored = [sem(f"stored{q}") for q in range(2)]
    back = BackwardScan(nc, m, sem, xc_ready)

    with nc.Block() as block:
        @block.vector
        def _(v):
            for h in range(2):
                last = v.tensor_scalar(crow[:, h, :], m.ones[:, :], m.coef[:, 2, h:h + 1], None, ALU.mult)
            last.then_inc(c_ready, 1)
            back.init(v)
            v.wait_ge(c_ps, 1)
            v.tensor_copy(c_out[:, :], ps[:, 4, 0:D]).then_inc(cout_ready, 1)

            def fill(j, q, turn):
                back.fill(v, j, q)

            def back_scan(j, q, turn):
                back.scan(v, j, q)

            staged(v, CHUNKS, 2, (0, back_scan), (1, fill))

        @block.gpsimd
        def _(g):
            g.sem_inc(kept.sem, kept.ahead)

            def keep(j, q, turn):
                g.wait_ge(xc_ready.sem, xc_ready.done(j))
                settle(g, m)
                g.tensor_copy(m.feat[:, :, bass.ds(from_end(j) * CW + 1, CW)], xc[:, q, :, :]).then_inc(kept.sem, 1)

            staged(g, CHUNKS, 2, (0, keep))

        @block.scalar
        def _(a):
            a.sem_inc(rows_ready.sem, rows_ready.ahead)
            a.sem_inc(xc_ready.sem, xc_ready.ahead)

            def features(j, q, turn):
                a.wait_ge(back.done, back.scanned(j))
                a.wait_ge(rows_ps.sem, rows_ps.free(j, 2))
                a.wait_ge(kept.sem, kept.free(j, 2))
                for h in range(2):
                    last = a.activation(xc[:, q, h, :], back.vals[:, q, h, :], ACT.Relu,
                                        bias=m.coef[:, 1, h:h + 1], scale=m.coef[:, 0, h:h + 1])
                last.then_inc(xc_ready.sem, 1)

            def copy_rows(j, q, turn):
                a.wait_ge(rows_ps.sem, rows_ps.done(j))
                a.wait_ge(stored[q], turn * 16)
                a.activation(rows[:, q, :, :].rearrange("p u k -> p (u k)"), ps[:, q, :], ACT.Copy).then_inc(rows_ready.sem, 1)

            staged(a, CHUNKS, 2, (1, features), (0, copy_rows))

        @block.tensor
        def _(pe):
            pe.sem_inc(rows_ps.sem, rows_ps.ahead)
            pe.wait_ge(c_ready, 1)
            for kh in range(2):
                last = pe.matmul(ps[:, 4, 0:D], crow[:, kh, :], m.wt[:, l, 0, kh, :], start=(kh == 0), stop=(kh == 1))
            last.then_inc(c_ps, 1)

            def products(j, q, turn):
                pe.wait_ge(xc_ready.sem, xc_ready.done(j))
                pe.wait_ge(rows_ready.sem, rows_ready.free(j, 2))
                for u in range(2):
                    for kh in range(2):
                        last = pe.matmul(ps[:, q, u * D:u * D + D], xc[:, q, kh, u * P:u * P + P], m.wt[:, l, 0, kh, :],
                                         start=(kh == 0), stop=(kh == 1))
                last.then_inc(rows_ps.sem, 1)

            staged(pe, CHUNKS, 2, (0, products))

        @block.sync
        def _(sp):
            sp.wait_ge(cout_ready, 1)
            sp.dma_start(m.projected[CROW:CROW + P, :], c_out[:, :]).then_inc(cout_done, 16)

            def store(j, q, turn):
                sp.wait_ge(rows_ready.sem, rows_ready.done(j))
                settle(sp, m)
                sp.dma_start(m.projected[bass.ds(from_end(j) * CW, CW), :].rearrange("(u p) k -> p u k", p=P),
                             rows[:, q, :, :]).then_inc(stored[q], 16)

            staged(sp, CHUNKS, 2, (0, store))
            sp.wait_ge(cout_done, 16)
            for q in range(2):
                sp.wait_ge(stored[q], CHUNKS // 2 * 16)


def messages(nc, m):
    sb, ps = m.sb, m.psum
    sem = lambda n: m.sem(f"{n}_m")
    xc = sb("xc_m", [P, 2, CW], F32)
    LD = 4
    ld = sb("ld", [P, LD, 2, C_S - C_X], F32)
    used_up = m.wt.rearrange("p l s k o -> p (l s k o)")
    xp = used_up[:, 8 * CW:8 * CW + 4 * D].rearrange("p (q u k) -> p q u k", q=2, u=2)
    xb = sb("xb", [P, LD, 2, D], F32)
    hg = sb("hg", [P, 2, 2, 2, D], F32)
    hgT = used_up[:, 0:8 * CW].rearrange("p (q s k e) -> p q s k e", q=2, s=2, k=2)
    res = sb("res", [P, 2, 2, 2, D], F32)
    stats = sb("stats_m", [P, 2, 6], F32)
    mv = sb("mv_m", [P, 2, 2], F32)
    std = sb("std_m", [P, 2], F32)
    rstd = sb("rstd_m", [P, 2], F32)
    nmr = sb("nmr_m", [P, 2], F32)
    first = sb("first", [P, 1], BF16)
    x_ps, xp_ready, mv_ready, std_ready, ln_ready, first_ready, dve_own = (
        sem(n) for n in ("x_ps", "xp_ready", "mv_ready", "std_ready", "ln_ready", "first_ready", "dve_own"))
    xc_ready, h_ready, xb_ready, hgT_ps, hgT_ready, out_ps, out_ready, y_ready = (
        Signal(sem(n), 1) for n in ("xc_ready", "h_ready", "xb_ready", "hgT_ps", "hgT_ready", "out_ps", "out_ready", "y_ready"))
    g_ready = Signal(sem("g_ready"), LD - 1)
    out_ready = Signal(out_ready.sem, LD - 1)
    loaded = [sem(f"loaded{q}") for q in range(LD)]
    stored = [sem(f"stored{q}") for q in range(2)]
    back = BackwardScan(nc, m, sem, xc_ready)

    with nc.Block() as block:
        @block.sync
        def _(sp):
            def load(j, q, turn):
                sp.wait_ge(g_ready.sem, g_ready.free(j, LD))
                settle(sp, m)
                sp.dma_start(ld[:, q, :, :], m.sorted[bass.ds(from_end(j) * CW, CW), C_X:C_S]
                             .rearrange("(u p) w -> p u w", p=P)).then_inc(loaded[q], 16)

            def store(j, q, turn):
                sp.wait_ge(y_ready.sem, y_ready.done(j))
                settle(sp, m)
                for w, table in enumerate((m.rewritten, m.messages)):
                    sp.dma_start(table[bass.ds(from_end(j) * CW, CW), :].rearrange("(u p) k -> p u k", p=P),
                                 res[:, q % 2, w, :, :]).then_inc(stored[q % 2], 16)

            staged(sp, CHUNKS, LD, (5, load), (0, store))
            for q in range(2):
                sp.wait_ge(stored[q], CHUNKS // 2 * 32)

        @block.gpsimd
        def _(g):
            g.sem_inc(g_ready.sem, g_ready.ahead)
            g.sem_inc(xb_ready.sem, xb_ready.ahead)

            def times_relation(j, q, turn):
                g.wait_ge(h_ready.sem, h_ready.done(j))
                g.wait_ge(hgT_ps.sem, hgT_ps.free(j, 2))
                g.tensor_tensor(hg[:, q % 2, 1, :, :], hg[:, q % 2, 0, :, :], ld[:, q, :, D:2 * D], ALU.mult).then_inc(g_ready.sem, 1)

            def plus_bias(j, q, turn):
                g.wait_ge(xp_ready, j + 1)
                g.wait_ge(out_ready.sem, out_ready.free(j, LD))
                for u in range(2):
                    last = g.tensor_tensor(xb[:, q, u, :], xp[:, q % 2, u, :], m.updb[:, :], ALU.add)
                last.then_inc(xb_ready.sem, 1)

            staged(g, CHUNKS, LD, (2, times_relation), (2, plus_bias))

        @block.scalar
        def _(a):
            a.sem_inc(h_ready.sem, h_ready.ahead)
            a.sem_inc(xc_ready.sem, xc_ready.ahead)
            a.sem_inc(hgT_ready.sem, hgT_ready.ahead)
            a.sem_inc(y_ready.sem, y_ready.ahead)

            def features(j, q, turn):
                a.wait_ge(back.done, back.scanned(j))
                a.wait_ge(x_ps, j)
                for h in range(2):
                    last = a.activation(xc[:, h, :], back.vals[:, q, h, :], ACT.Relu,
                                        bias=m.coef[:, 1, h:h + 1], scale=m.coef[:, 0, h:h + 1])
                last.then_inc(xc_ready.sem, 1)

            def normalise(j, q, turn):
                a.wait_ge(ln_ready, j + 1)
                a.wait_ge(hgT_ps.sem, hgT_ps.free(j, 2))
                for u in range(2):
                    last = a.activation(hg[:, q, 0, u, :], xp[:, q, u, :], ACT.Relu, bias=nmr[:, u:u + 1], scale=rstd[:, u:u + 1])
                last.then_inc(h_ready.sem, 1)

            def transposed(j, q, turn):
                a.wait_ge(hgT_ps.sem, hgT_ps.done(j))
                a.wait_ge(out_ps.sem, out_ps.free(j, 2))
                for s in range(2):
                    last = a.activation(hgT[:, q, s, :, :].rearrange("p k e -> p (k e)"), ps[:, 1 + s, :], ACT.Copy)
                last.then_inc(hgT_ready.sem, 1)

            def root(j, q, turn):
                a.wait_ge(mv_ready, j + 1)
                a.activation(std[:, :], mv[:, :, 1], ACT.Sqrt, bias=m.eps[:, :]).then_inc(std_ready, 1)

            def scale(j, q, turn):
                a.wait_ge(out_ready.sem, out_ready.done(j))
                for u in range(2):
                    y = res[:, q, 1, u, :]
                    last = a.activation(y, y, ACT.Copy, scale=m.meta[:, bass.ds(from_end(j) * 2 + u, 1), 0])
                last.then_inc(y_ready.sem, 1)

            staged(a, CHUNKS, 2, (1, transposed), (2, normalise), (3, root), (4, features), (0, scale))

        @block.tensor
        def _(pe):
            pe.sem_inc(hgT_ps.sem, hgT_ps.ahead)
            pe.sem_inc(out_ps.sem, out_ps.ahead)
            pe.wait_ge(first_ready, 1)

            def turn_x(j, q, turn):
                pe.wait_ge(xc_ready.sem, xc_ready.done(j))
                pe.wait_ge(xp_ready, j)
                for u in range(2):
                    for h in range(2):
                        last = pe.transpose(ps[:, 0, u * D + h * P:u * D + h * P + P], xc[:, h, u * P:u * P + P], m.ident[:, :])
                last.then_inc(x_ps, 1)

            def turn_h(j, q, turn):
                pe.wait_ge(h_ready.sem, h_ready.done(j))
                pe.wait_ge(g_ready.sem, g_ready.done(j))
                pe.wait_ge(hgT_ready.sem, hgT_ready.free(j, 1))
                for s in range(2):
                    for kh in range(2):
                        for u in range(2):
                            last = pe.transpose(ps[:, 1 + s, kh * CW + u * P:kh * CW + u * P + P],
                                                hg[:, q, s, u, kh * P:kh * P + P], m.ident[:, :])
                last.then_inc(hgT_ps.sem, 1)

            def products(j, q, turn):
                pe.wait_ge(hgT_ready.sem, hgT_ready.done(j))
                pe.wait_ge(out_ready.sem, out_ready.free(j, 2))
                for u in range(2):
                    pe.matmul(ps[:, 7, bass.ds(from_end(j) * 2 + u, 1)], m.same[:, bass.ds(from_end(j) * CW + (u * P + 1), P)],
                              first[:, :], start=True, stop=True)
                for s, w in enumerate((m.upd, m.msg)):
                    for u in range(2):
                        for kh in range(2):
                            last = pe.matmul(ps[:, 3 + 2 * q + s, u * D:u * D + D], hgT[:, q, s, kh, u * P:u * P + P], w[:, kh, :],
                                             start=(kh == 0), stop=(kh == 1))
                last.then_inc(out_ps.sem, 1)

            staged(pe, CHUNKS, 2, (1, turn_h), (0, products), (4, turn_x))

        @block.vector
        def _(v):
            chain = Chain(v, dve_own)
            v.sem_inc(out_ready.sem, out_ready.ahead)
            back.init(v)
            v.tensor_copy(first[:, :], m.identb[:, 0:1]).then_inc(first_ready, 1)

            def fill(j, q, turn):
                back.fill(v, j, q % 2)

            def back_scan(j, q, turn):
                back.scan(v, j, q % 2)

            def statistics(j, q, turn):
                v.wait_ge(x_ps, j + 1)
                v.wait_ge(loaded[q], (turn + 1) * 16)
                v.wait_ge(h_ready.sem, h_ready.free(j, 2))
                v.wait_ge(xb_ready.sem, xb_ready.free(j, 2))
                v.tensor_tensor(xp[:, q % 2, :, :], ps[:, 0, :].rearrange("p (u k) -> p u k", u=2), ld[:, q, :, 0:D], ALU.add).then_inc(xp_ready, 1)
                v.wait_ge(xp_ready, j + 1)
                for u in range(2):
                    last = v.bn_stats(stats[:, u, :], xp[:, q % 2, u, :])
                chain(last)
                settle(v, m)
                for u in range(2):
                    last = v.bn_aggr(mv[:, u, :], stats[:, u, :])
                last.then_inc(mv_ready, 1)

            def scales(j, q, turn):
                v.wait_ge(std_ready, j + 1)
                v.wait_ge(h_ready.sem, h_ready.free(j, 1))
                chain(v.reciprocal(rstd[:, :], std[:, :]))
                v.scalar_tensor_tensor(nmr[:, :], mv[:, :, 0], -1.0, rstd[:, :], ALU.mult, ALU.mult).then_inc(ln_ready, 1)

            def results(j, q, turn):
                half, slot, q = q // 2, q, q % 2
                v.wait_ge(out_ps.sem, out_ps.done(j))
                v.wait_ge(xb_ready.sem, xb_ready.done(j))
                v.wait_ge(y_ready.sem, y_ready.free(j, 2))
                v.wait_ge(stored[q], (turn * (LD // 2) + half) * 32)
                v.tensor_tensor(res[:, q, 0, :, :], ps[:, 3 + 2 * q, :].rearrange("p (u k) -> p u k", u=2), xb[:, slot, :, :], ALU.add)
                for u in range(2):
                    last = v.tensor_tensor(res[:, q, 1, u, :], ps[:, 4 + 2 * q, u * D:u * D + D], m.msgb[:, :], ALU.add)
                last.then_inc(out_ready.sem, 1)

            staged(v, CHUNKS, LD, (2, scales), (3, statistics), (4, back_scan), (5, fill), (0, results), chain=chain, counts=(1, 1, 0, 0, 0))
            v.wait_ge(out_ps.sem, out_ps.done(CHUNKS - 1))
            v.scalar_tensor_tensor(m.last_src[:, :], ps[:, 7, 0:TILES], float(2 * N), m.meta[:, :, 2], ALU.mult, ALU.add)


def all_nodes(nc, m):
    sb, ps = m.sb, m.psum
    sem = lambda n: m.sem(f"{n}_d")
    G = 4
    ROWS = G * P
    TURNS = -(-N // ROWS)
    XS = 6
    xp = sb("xp_d", [P, 2, G, D], F32)
    xb = sb("xb_d", [P, 2, G, D], F32)
    big = m.big
    h = big[:, 0:2 * G * D].rearrange("p (q g k) -> p q g k", q=2, g=G)
    hT = big[:, 2048:2048 + 2 * G * D].rearrange("p (q g k) -> p q g k", q=2, g=G)
    res = big[:, 4096:4096 + 2 * G * D].rearrange("p (q g k) -> p q g k", q=2, g=G)
    cb = big[:, 6200:6200 + 2 * G * D].rearrange("p (w g k) -> p w g k", w=2, g=G)
    diag = big[:, 8300:8300 + D].rearrange("p (h k) -> p h k", h=2)
    xs = big[:, 8600:8600 + XS * G * D].rearrange("p (q g k) -> p q g k", q=XS, g=G)
    stats = sb("stats_d", [P, G, 6], F32)
    mv = sb("mv_d", [P, 2, G, 2], F32)
    std = sb("std_d", [P, G], F32)
    rstd = sb("rstd_d", [P, 2, G], F32)
    nmr = sb("nmr_d", [P, 2, G], F32)
    c_ready, c_ps, cb_ready, mv_ready, std_ready, ln_ready, dve_own = (
        sem(n) for n in ("c_ready", "c_ps", "cb_ready", "mv_ready", "std_ready", "ln_ready", "dve_own"))
    xp_ready, xb_ready, hT_ready, res_ready = (
        Signal(sem(n), a) for n, a in (("xp_ready", XS - 1), ("xb_ready", XS - 1), ("hT_ready", 1), ("res_ready", 1)))
    h_ready, hT_ps, out_ps = (Signal(sem(n), 1) for n in ("h_ready", "hT_ps", "out_ps"))
    loaded = [sem(f"loaded{q}") for q in range(6)]
    stored = [sem(f"stored{q}") for q in range(2)]
    SLOTS = XS

    def at(c):
        return N - ROWS if isinstance(c, int) and c == TURNS - 1 else c * ROWS

    with nc.Block() as block:
        @block.sync
        def _(sp):
            def load(c, q, turn):
                sp.wait_ge(xp_ready.sem, xp_ready.free(c, XS))
                sp.wait_ge(xb_ready.sem, xb_ready.free(c, XS))
                sp.dma_start(xs[:, q, :, :], m.x[bass.ds(at(c), ROWS), :].rearrange("(p g) k -> p g k", g=G)).then_inc(loaded[q], 16)

            def store(c, q, turn):
                if isinstance(c, int) and c == TURNS - 1:
                    sp.wait_ge(stored[1 - q % 2], (TURNS // 2) * 16)
                sp.wait_ge(res_ready.sem, res_ready.done(c))
                sp.dma_start(m.out[bass.ds(at(c), ROWS), :].rearrange("(p g) k -> p g k", g=G), res[:, q % 2, :, :]).then_inc(stored[q % 2], 16)

            staged(sp, TURNS, SLOTS, (5, load), (0, store), peel=1)
            sp.wait_ge(stored[0], (TURNS + 1) // 2 * 16)
            sp.wait_ge(stored[1], TURNS // 2 * 16)

        @block.gpsimd
        def _(g):
            g.sem_inc(xb_ready.sem, xb_ready.ahead)
            g.wait_ge(cb_ready, 1)

            def bias(c, q, turn):
                g.wait_ge(loaded[q], (turn + 1) * 16)
                g.wait_ge(res_ready.sem, res_ready.free(c, 2))
                g.tensor_tensor(xb[:, q % 2, :, :], xs[:, q, :, :], cb[:, 1, :, :], ALU.add).then_inc(xb_ready.sem, 1)

            staged(g, TURNS, SLOTS, (0, bias))

        @block.scalar
        def _(a):
            a.sem_inc(hT_ready.sem, hT_ready.ahead)
            a.sem_inc(h_ready.sem, h_ready.ahead)
            for k in range(2):
                last = a.activation(diag[:, k, :], m.ident[:, :], ACT.Copy, scale=m.coef[:, 2, k:k + 1])
            last.then_inc(c_ready, 1)

            def normalise(c, q, turn):
                q = q % 2
                a.wait_ge(ln_ready, c + 1)
                a.wait_ge(hT_ps.sem, hT_ps.free(c, 2))
                for n in range(G):
                    last = a.activation(h[:, q, n, :], xp[:, q, n, :], ACT.Relu, bias=nmr[:, q, n:n + 1], scale=rstd[:, q, n:n + 1])
                last.then_inc(h_ready.sem, 1)

            def transposed(c, q, turn):
                q = q % 2
                a.wait_ge(hT_ps.sem, hT_ps.done(c))
                a.wait_ge(out_ps.sem, out_ps.free(c, 2))
                for b in range(2):
                    last = a.activation(hT[:, q, 2 * b:2 * b + 2, :], ps[:, 2 * q + b, :].rearrange("p (g k) -> p g k", g=2), ACT.Copy)
                last.then_inc(hT_ready.sem, 1)

            def root(c, q, turn):
                a.wait_ge(mv_ready, c + 1)
                a.activation(std[:, :], mv[:, q % 2, :, 1], ACT.Sqrt, bias=m.eps[:, :]).then_inc(std_ready, 1)

            staged(a, TURNS, SLOTS, (1, transposed), (2, normalise), (3, root))

        @block.tensor
        def _(pe):
            pe.sem_inc(hT_ps.sem, hT_ps.ahead)
            pe.sem_inc(out_ps.sem, out_ps.ahead)
            pe.wait_ge(c_ready, 1)
            pe.matmul(ps[:, 4, 0:D], m.ones[:, :], diag[:, :, :].rearrange("p h k -> p (h k)"), start=True, stop=True).then_inc(c_ps, 1)

            def turn_h(c, q, turn):
                q = q % 2
                pe.wait_ge(h_ready.sem, h_ready.done(c))
                pe.wait_ge(hT_ready.sem, hT_ready.free(c, 2))
                for n in range(G):
                    for kh in range(2):
                        last = pe.transpose(ps[:, 2 * q + n // 2, (n % 2) * D + kh * P:(n % 2) * D + kh * P + P],
                                            h[:, q, n, kh * P:kh * P + P], m.ident[:, :])
                last.then_inc(hT_ps.sem, 1)

            def products(c, q, turn):
                q = q % 2
                pe.wait_ge(hT_ready.sem, hT_ready.done(c))
                pe.wait_ge(res_ready.sem, res_ready.free(c, 2))
                for n in range(G):
                    for kh in range(2):
                        last = pe.matmul(ps[:, 4 + 2 * q + n // 2, (n % 2) * D:(n % 2) * D + D], hT[:, q, n, kh * P:kh * P + P],
                                         m.upd[:, kh, :], start=(kh == 0), stop=(kh == 1))
                last.then_inc(out_ps.sem, 1)

            pe.wait_ge(cb_ready, 1)
            staged(pe, TURNS, SLOTS, (1, turn_h), (0, products))

        @block.vector
        def _(v):
            chain = Chain(v, dve_own)
            v.sem_inc(xp_ready.sem, xp_ready.ahead)
            v.sem_inc(res_ready.sem, res_ready.ahead)
            v.wait_ge(c_ps, 1)
            for n in range(G):
                v.tensor_copy(cb[:, 0, n, :], ps[:, 4, 0:D])
                last = v.tensor_tensor(cb[:, 1, n, :], ps[:, 4, 0:D], m.updb[:, :], ALU.add)
            last.then_inc(cb_ready, 1)
            v.wait_ge(cb_ready, 1)

            def statistics(c, q, turn):
                v.wait_ge(loaded[q], (turn + 1) * 16)
                v.wait_ge(h_ready.sem, h_ready.free(c, 2))
                v.tensor_tensor(xp[:, q % 2, :, :], xs[:, q, :, :], cb[:, 0, :, :], ALU.add).then_inc(xp_ready.sem, 1)
                v.wait_ge(xp_ready.sem, xp_ready.done(c))
                q = q % 2
                for n in range(G):
                    last = v.bn_stats(stats[:, n, :], xp[:, q, n, :])
                chain(last)
                settle(v, m)
                for n in range(G):
                    last = v.bn_aggr(mv[:, q, n, :], stats[:, n, :])
                last.then_inc(mv_ready, 1)

            def scales(c, q, turn):
                q = q % 2
                v.wait_ge(std_ready, c + 1)
                chain(v.reciprocal(rstd[:, q, :], std[:, :]))
                v.scalar_tensor_tensor(nmr[:, q, :], mv[:, q, :, 0], -1.0, rstd[:, q, :], ALU.mult, ALU.mult).then_inc(ln_ready, 1)

            def results(c, q, turn):
                earlier = (turn * (SLOTS // 2) + q // 2) * 16
                q = q % 2
                v.wait_ge(out_ps.sem, out_ps.done(c))
                v.wait_ge(xb_ready.sem, xb_ready.done(c))
                v.wait_ge(stored[q], earlier)
                for b in range(2):
                    last = v.tensor_tensor(res[:, q, 2 * b:2 * b + 2, :], ps[:, 4 + 2 * q + b, :].rearrange("p (g k) -> p g k", g=2),
                                           xb[:, q, 2 * b:2 * b + 2, :], ALU.add)
                last.then_inc(res_ready.sem, 1)

            staged(v, TURNS, SLOTS, (2, scales), (3, statistics), (0, results), chain=chain, counts=(1, 1, 0))


def rewrite_sources(nc, m):
    sb = m.sb
    sem = lambda n: m.sem(f"{n}_w")
    SLOTS = 6
    rows = [sb(f"rows_w{q}", [P, D], F32) for q in range(SLOTS)]
    idx = [sb(f"idx_w{q}", [P, 1], I32) for q in range(SLOTS)]
    idx_ready = sem("idx_ready")
    issued = Signal(sem("issued"), SLOTS - 1)
    loaded = [sem(f"loaded{q}") for q in range(SLOTS)]
    scattered = [sem(f"scattered{q}") for q in range(SLOTS)]

    with nc.Block() as block:
        @block.sync
        def _(sp):
            def load(t, q, turn):
                sp.wait_ge(scattered[q], turn * 16)
                sp.dma_start(rows[q][:, :], m.rewritten[bass.ds(t * P, P), :]).then_inc(loaded[q], 16)

            staged(sp, TILES, SLOTS, (0, load))

        @block.gpsimd
        def _(g):
            def scatter(t, q, turn):
                g.wait_ge(loaded[q], (turn + 1) * 16)
                g.tensor_copy(idx[q][:, :], m.last_src[:, bass.ds(t, 1)]).then_inc(idx_ready, 1)
                g.wait_ge(idx_ready, t + 1)
                settle(g, m)
                g.indirect_dma_start(out=m.out, out_offset=bass.IndirectOffsetOnAxis(ap=idx[q][:, :], axis=0),
                                     in_=rows[q][:, :], in_offset=None, bounds_check=N - 1, oob_is_err=False).then_inc(scattered[q], 16)

            staged(g, TILES, SLOTS, (0, scatter))
            for q in range(SLOTS):
                g.wait_ge(scattered[q], len(range(q, TILES, SLOTS)) * 16)


def add_messages(nc, m):
    sb, ps = m.sb, m.psum
    sem = lambda n: m.sem(f"{n}_a")
    SLOTS = 4
    rows = [sb(f"rows_a{q}", [P, D], F32) for q in range(SLOTS)]
    gi = [sb(f"gi_a{q}", [P, 1], I32) for q in range(SLOTS)]
    idx = [sb(f"idx_a{q}", [P, 1], I32) for q in range(SLOTS)]
    sums = [sb(f"sums_a{q}", [P, D], F32) for q in range(SLOTS)]
    keys = sb("keys_a", [P, SLOTS, P], I32)
    equal = sb("equal", [P, SLOTS, P], F32)
    junk = sb("junk_a", [P, SLOTS, P], BF16)
    before = sb("before_a", [P, SLOTS], F32)
    dump = sb("dump", [P, 1], F32)
    t1 = sb("t1_a", [P, SLOTS, 2], F32)
    dumpi = sb("dumpi", [P, 1], I32)
    gi_ready, dump_ready, equal_ready, sum_ps, sum_ready, dve_own = (
        sem(n) for n in ("gi_ready", "dump_ready", "equal_ready", "sum_ps", "sum_ready", "dve_own"))
    added = [sem(f"added{q}") for q in range(SLOTS)]
    gathered = [sem(f"gathered{q}") for q in range(SLOTS)]
    keys_in = [sem(f"keys_in{q}") for q in range(SLOTS)]

    with nc.Block() as block:
        @block.sync
        def _(sp):
            def load_keys(t, q, turn):
                sp.wait_ge(equal_ready, turn * SLOTS)
                sp.dma_start(keys[:, q, :], bass.AP(tensor=m.dkeys.tensor, offset=t * P, ap=[[0, P], [1, P]])).then_inc(keys_in[q], 16)

            staged(sp, TILES, SLOTS, (0, load_keys))

        @block.gpsimd
        def _(g):
            g.iota(dumpi[:, :], pattern=[[0, 1]], base=N, channel_multiplier=1).then_inc(dump_ready, 1)

            def gather(t, q, turn):
                g.wait_ge(sum_ps, turn * SLOTS)
                g.tensor_copy(gi[q][:, :], m.ranks[:, bass.ds(t, 1)]).then_inc(gi_ready, 1)
                g.wait_ge(gi_ready, t + 1)
                settle(g, m)
                g.indirect_dma_start(out=rows[q][:, :], out_offset=None, in_=m.messages,
                                     in_offset=bass.IndirectOffsetOnAxis(ap=gi[q][:, :], axis=0)).then_inc(gathered[q], 16)

            def add(t, q, turn):
                g.wait_ge(sum_ready, t + 1)
                g.wait_ge(added[(q - 1) % SLOTS], (turn + (q > 0)) * 16)
                settle(g, m)
                g.indirect_dma_start(out=m.out, out_offset=bass.IndirectOffsetOnAxis(ap=idx[q][:, :], axis=0),
                                     in_=sums[q][:, :], in_offset=None, compute_op=ALU.add).then_inc(added[q], 16)

            staged(g, TILES, SLOTS, (2, gather), (0, add))
            g.wait_ge(added[(TILES - 1) % SLOTS], TILES // SLOTS * 16)

        @block.tensor
        def _(pe):
            def sum_equal(t, q, turn):
                pe.wait_ge(equal_ready, t + 1)
                pe.wait_ge(gathered[q], (turn + 1) * 16)
                pe.wait_ge(sum_ready, t)
                pe.matmul(ps[:, 0, 0:D], equal[:, q, :], rows[q][:, :], start=True, stop=True).then_inc(sum_ps, 1)

            staged(pe, TILES, SLOTS, (0, sum_equal))

        @block.vector
        def _(v):
            chain = Chain(v, dve_own)
            v.wait_ge(dump_ready, 1)
            chain(v.tensor_copy(dump[:, :], dumpi[:, :]))

            def edges(t, q, turn):
                dst = m.dstf[:, bass.ds(t, 1)]
                v.wait_ge(keys_in[q], (turn + 1) * 16)
                v.wait_ge(sum_ps, turn * SLOTS)
                v.scalar_tensor_tensor(junk[:, q, :], keys[:, q, :], dst, m.earlier[:, 0, 0:P], ALU.is_equal, ALU.mult,
                                       accum_out=before[:, q:q + 1])
                v.tensor_scalar(equal[:, q, :], keys[:, q, :], dst, None, ALU.is_equal).then_inc(equal_ready, 1)
                v.wait_ge(equal_ready, t + 1)
                v.tensor_tensor(t1[:, q, 0:1], dst, dump[:, :], ALU.subtract)
                chain(v.tensor_scalar(t1[:, q, 1:2], dst, float(N), None, ALU.is_lt))
                chain(v.tensor_tensor(t1[:, q, 0:1], t1[:, q, 0:1], t1[:, q, 1:2], ALU.mult))
                chain(v.scalar_tensor_tensor(t1[:, q, 0:1], before[:, q:q + 1], 0.0, t1[:, q, 0:1], ALU.is_equal, ALU.mult))
                v.wait_ge(added[q], turn * 16)
                chain(v.tensor_tensor(idx[q][:, :], t1[:, q, 0:1], dump[:, :], ALU.add))

            def copy_sums(t, q, turn):
                v.wait_ge(sum_ps, t + 1)
                v.tensor_copy(sums[q][:, :], ps[:, 0, 0:D]).then_inc(sum_ready, 1)

            staged(v, TILES, SLOTS, (1, edges), (0, copy_sums), chain=chain, counts=(4, 0))


_INS = ['x', 'src', 'dst', 'edge_type_500', 'L0_gnn_thetas', 'L0_gnn_phis', 'L0_gnn_gammas', 'L0_gnn_betas',
        'L1_gnn_relation_emb', 'L1_gnn_msg_w', 'L1_gnn_msg_b', 'L1_gnn_upd_w', 'L1_gnn_upd_b', 'L1_gnn_gate_w', 'L1_gnn_gate_b']
OUT_ROWS = N + P


def kernel(**inputs):
    import numpy as _np
    import concourse.bacc as _bacc
    from concourse import mybir as _mybir
    from concourse.bass_utils import run_bass_kernel_spmd as _run

    nc = _bacc.Bacc("TRN2", target_bir_lowering=False, num_devices=1)
    arrays, args = {}, []
    for name in _INS:
        a = _np.ascontiguousarray(inputs[name])
        arrays[f"in_{name}"] = a
        args.append(nc.dram_tensor(f"in_{name}", a.shape, _mybir.dt.from_np(a.dtype), kind="ExternalInput").ap())
    args.append(nc.dram_tensor("out_0", (OUT_ROWS, D), _mybir.dt.float32, kind="ExternalOutput").ap())
    program(nc, *args)
    r = _run(nc, [arrays], core_ids=[0])
    return r.results[0]["out_0"][:N]
```

```python
import concourse.bass as bass
from concourse import mybir
from contextlib import ExitStack

F32 = mybir.dt.float32
BF16 = mybir.dt.bfloat16
I32 = mybir.dt.int32
ALU = mybir.AluOpType
ACT = mybir.ActivationFunctionType

P = 128
N = 50000
D = 256
E = 12500
R = 500
L = 3
TILES = 100
CHUNKS = TILES // 2
EP = TILES * P
CW = 2 * P
LAST = E // P
LASTN = E - LAST * P
LO = 256
PAD_KEY = 195 * LO + 255
CROW = EP
EPS = 1e-5
RT = 125

C_E, C_X, C_META, SW = 0, D, 2 * D, 2 * D + 8
M_SCALE, M_SRC, M_DST, M_TYPE, M_POS, M_IN, METAS = 0, 1, 2, 3, 4, 5, 8


class Program:
    pass


class Chain:

    def __init__(self, eng, sem):
        self.eng, self.sem, self.base, self.i, self.per, self.k = eng, sem, 0, 0, 0, 0

    def loop(self, i, per):
        self.base, self.i, self.per, self.k = self.base + self.k, i, per, 0

    def end(self, iters):
        assert self.k == self.per, (self.k, self.per)
        self.base, self.i, self.per, self.k = self.base + iters * self.per, 0, 0, 0

    def __call__(self, ins):
        ins.then_inc(self.sem, 1)
        self.k += 1
        self.eng.wait_ge(self.sem, self.i * self.per + (self.base + self.k))


class Signal:

    def __init__(self, sem, ahead):
        self.sem, self.ahead = sem, ahead

    def done(self, c):
        return c + (1 + self.ahead)

    def free(self, c, slots):
        assert self.ahead >= slots - 1
        return c + (1 + self.ahead - slots)


def staged(eng, total, slots, *steps, chain=None, counts=(), peel=0):
    ahead = max(a for a, _ in steps)

    def at(s):
        for a, step in steps:
            if 0 <= s + a < total:
                step(s + a, (s + a) % slots, (s + a) // slots)

    loops = (total - ahead - peel) // slots - 1
    for s in range(-ahead, slots):
        at(s)
    with eng.Fori(0, loops) as i:
        if chain:
            chain.loop(i, sum(counts) * slots)
        for u in range(slots, 2 * slots):
            for a, step in steps:
                step(i * slots + (u + a), (u + a) % slots, i + (u + a) // slots)
        if chain:
            chain.end(loops)
    for s in range((loops + 1) * slots, total):
        at(s)


def settle(eng, m):
    eng.sem_inc(m.settled, 1)


def row_broadcast(v, rows, cols):
    return bass.AP(tensor=v.tensor, offset=v.offset, ap=[[0, rows], [1, cols]])


def program(nc, x, src, dst, typ, thetas, phis, gammas, betas, rel, msg_w, msg_b, upd_w, upd_b, gate_w, gate_b, out):
    ctx = ExitStack()
    with ctx:
        def sb(name, shape, dt):
            return ctx.enter_context(nc.sbuf_tensor(name, shape, dt))

        def dram(name, shape, dt):
            return nc.dram_tensor(name, shape, dt, kind="Internal").ap()

        m = Program()
        m.x, m.src, m.dst, m.typ, m.thetas, m.phis, m.gammas, m.betas = x, src, dst, typ, thetas, phis, gammas, betas
        m.rel, m.msg_w, m.msg_b, m.upd_w, m.upd_b, m.gate_w, m.gate_b, m.out = rel, msg_w, msg_b, upd_w, upd_b, gate_w, gate_b, out
        m.node_table = dram("node_table", (2 * P * LO, 2), I32)
        m.relations = dram("relations", (EP, D), F32)
        m.rel_table = dram("rel_table", (R, D + 1), F32)
        m.keys = dram("keys", (EP,), I32)
        m.sorted = dram("sorted_edges", (EP, SW), F32)
        m.settled = ctx.enter_context(nc.semaphore("settled"))
        m.projected = dram("projected", (EP + P, D), F32)
        m.messages = dram("messages", (EP, D), F32)
        m.placed_dst = dram("placed_dst", (EP,), F32)
        m.ident = sb("ident", [P, P], F32)
        m.identb = sb("identb", [P, P], BF16)
        m.ones = sb("ones", [P, P], F32)
        m.before = sb("before", [P, P], F32)
        m.iota = sb("iota", [P, LO], BF16)
        m.earlier = sb("earlier", [P, 2, CW], BF16)
        m.eps = sb("eps", [P, 1], F32)
        m.zerob = sb("zerob", [P, LO], BF16)
        m.wt = sb("wt", [P, L, 2, 2, D], F32)
        m.upd = sb("upd", [P, 2, D], F32)
        m.msg = sb("msg", [P, 2, D], F32)
        m.updb = sb("updb", [P, D], F32)
        m.msgb = sb("msgb", [P, D], F32)
        m.gam = sb("gam", [P, L, 2], F32)
        m.bet = sb("bet", [P, L, 2], F32)
        m.srcf = sb("srcf", [P, TILES], F32)
        m.hl = sb("hl", [P, 4, TILES], F32)
        m.numbers = sb("numbers", [P, TILES, 3], F32)
        m.gidx = sb("gidx", [P, 3, TILES], I32)
        m.big = sb("big", [P, 2 * (EP + 2)], F32)
        m.same = sb("same", [P, EP + 1], BF16)
        m.base = sb("base", [P, 2, 2, LO], BF16)
        m.cnt = sb("cnt", [P, 2, 2, LO], BF16)
        m.psum = ctx.enter_context(nc.psum_tensor("banks", [P, 8, 512], F32))
        m.feat = m.big[:, :].rearrange("p (h k) -> p h k", h=2)
        m.meta = sb("meta", [P, TILES, METAS], F32)
        m.last_src = sb("last_src", [P, TILES], I32)
        m.gates = sb("gates", [P, TILES], F32)
        m.sums = sb("sums", [P, 2, 2, CHUNKS], F32)
        m.coef = sb("coef", [P, 3, 2], F32)

        def run(stage, *layer):
            m.stage += 1
            sems = []

            def stage_sem(name):
                sems.append(nc.alloc_semaphore(name=f"{name}_{m.stage}"))
                return sems[-1]

            m.sem = stage_sem
            with ExitStack() as own:
                m.sb = lambda name, shape, dt: own.enter_context(nc.sbuf_tensor(f"{name}_{m.stage}", shape, dt))
                stage(nc, m, *layer)
            nc.clear_and_free_semaphores(sems)
            nc.all_engine_barrier()

        m.stage = -1
        run(setup)
        run(count_nodes)
        run(rank_and_layer0)
        run(scan_forward, 0)
        for l in range(1, L):
            run(project, l)
            run(scan_forward, l)
        run(all_nodes)
        run(messages)
        run(add_messages)


def setup(nc, m):
    sb, sem, ps = m.sb, m.sem, m.psum
    ids = sb("ids", [TILES, 3, P], I32)
    idf = sb("idf", [TILES, 3, P], F32)
    raw = m.big[:, 0:2 * 2 * L * D].rearrange("p (w l h k) -> p w l h k", w=2, l=L, h=2)
    cliff = m.big[:, 3072:3072 + 2 * 2 * D].rearrange("p (w h k) -> p w h k", w=2, h=2)
    relr = m.big[:, 4096:4096 + 4 * (D + 1)].rearrange("p (t k) -> p t k", t=4)
    rowb = m.big[:, 5200:5200 + 4 * D].rearrange("p (w k) -> p w k", w=4)
    bcol = m.big[:, 6300:6302]
    bcols = m.big[:, 6400:6400 + 2 * P].rearrange("p (h k) -> p h k", h=2)
    gz = m.big[:, 6700:6708]
    iotai = m.big[:, 7000:7000 + LO].bitcast(I32)
    idi = m.big[:, 8000:8000 + 6 * TILES].bitcast(I32).rearrange("p (w t) -> p w t", w=6)
    idc = m.big[:, 9000:9000 + 4 * TILES].rearrange("p (w t) -> p w t", w=4)
    init, ids_in, keys_out, w_in, c_in, b_in, r_in = (sem(n) for n in ("init", "ids_in", "keys_out", "w_in", "c_in", "b_in", "r_in"))
    consts, idf_ready, id_ps, wd_ready, w_ps, w_used, cl_ready, cl_ps = (
        sem(n) for n in ("consts", "idf_ready", "id_ps", "wd_ready", "w_ps", "w_used", "cl_ready", "cl_ps"))
    kup_ready, msg_ps, gate_z, gate_s, rel_out, bc_ready = (sem(n) for n in ("kup_ready", "msg_ps", "gate_z", "gate_s", "rel_out", "bc_ready"))
    dve_own, pool_own = sem("dve_own0"), sem("pool_own0")
    NEG = {(0, 3), (1, 2), (2, 3)}
    BLOCK = [[0, 1, 2, 3], [1, 0, 3, 2], [2, 3, 0, 1], [3, 2, 1, 0]]

    with nc.Block() as block:
        @block.gpsimd
        def _(g):
            chain = Chain(g, pool_own)
            g.memset(ids[:, 0:2, :], PAD_KEY)
            g.memset(ids[:, 2:3, :], 0).then_inc(init, 1)
            g.memset(m.ident[:, :], 0.0)
            g.memset(m.ones[:, :], 1.0)
            g.memset(m.earlier[:, :, :], 1.0)
            g.memset(m.zerob[:, :], 0.0)
            chain(g.memset(m.eps[:, :], EPS))
            g.affine_select(out=m.ident[:, :], in_=m.ident[:, :], compare_op=ALU.not_equal, fill=1.0,
                            base=0, pattern=[[-1, P]], channel_multiplier=1)
            g.affine_select(out=m.before[:, :], in_=m.ones[:, :], compare_op=ALU.is_gt, fill=0.0,
                            base=0, pattern=[[1, P]], channel_multiplier=-1)
            g.affine_select(out=m.earlier[:, :, :], in_=m.earlier[:, :, :], compare_op=ALU.is_gt, fill=0.0,
                            base=0, pattern=[[P, 2], [-1, CW]], channel_multiplier=1)
            g.iota(iotai, pattern=[[1, LO]], base=0, channel_multiplier=0).then_inc(consts, 1)

        @block.sync
        def _(sp):
            sp.wait_ge(init, 1)
            for w, v in enumerate((m.src, m.dst, m.typ)):
                sp.dma_start(ids[0:LAST, w, :], v[0:LAST * P].rearrange("(t p) -> t p", p=P)).then_inc(ids_in, 16)
                sp.dma_start(ids[LAST:LAST + 1, w, 0:LASTN],
                             v[LAST * P:E].rearrange("(a p) -> a p", a=1)).then_inc(ids_in, 16)
            sp.wait_ge(ids_in, 6 * 16)
            sp.dma_start(m.keys.rearrange("(t p) -> t p", p=P), ids[:, 0, :]).then_inc(keys_out, 16)
            for l in range(L):
                for w, v in enumerate((m.thetas, m.phis)):
                    sp.dma_start(raw[:, w, l, :, :], v[l].rearrange("(h p) k -> p h k", p=P)).then_inc(w_in, 16)
            for w, v in enumerate((m.msg_w, m.upd_w)):
                for a in range(4):
                    for b in range(4):
                        sp.dma_start(cliff[64 * (a % 2):64 * (a % 2) + 64, w, a // 2, 64 * b:64 * b + 64],
                                     v[BLOCK[a][b]]).then_inc(c_in, 16)
            sp.dma_start(relr[0:RT, :, 0:D], m.rel.rearrange("(t p) k -> p t k", p=RT)).then_inc(r_in, 16)
            sp.dma_start(rowb[:, 0, :], row_broadcast(m.gate_w[0], P, D)).then_inc(b_in, 16)
            sp.dma_start(rowb[:, 2, :], row_broadcast(m.upd_b.rearrange("a b -> (a b)"), P, D)).then_inc(b_in, 16)
            sp.dma_start(gz[:, 0:1], row_broadcast(m.gate_b, P, 1)).then_inc(b_in, 16)
            for h in range(2):
                sp.dma_start(bcol[:, h:h + 1], m.msg_b.rearrange("(h a) b -> h (a b)", h=2)[h].rearrange("(p o) -> p o", o=1)).then_inc(b_in, 16)
                for l in range(L):
                    sp.dma_start(m.gam[:, l, h:h + 1], m.gammas[l, h * P:(h + 1) * P].rearrange("(p o) -> p o", o=1)).then_inc(b_in, 16)
                    sp.dma_start(m.bet[:, l, h:h + 1], m.betas[l, h * P:(h + 1) * P].rearrange("(p o) -> p o", o=1)).then_inc(b_in, 16)
            sp.wait_ge(gate_s, 1)
            sp.dma_start(m.rel_table.rearrange("(t p) k -> p t k", p=RT), relr[0:RT, :, :]).then_inc(rel_out, 16)
            sp.wait_ge(rel_out, 16)
            sp.wait_ge(keys_out, 16)

        @block.vector
        def _(v):
            chain = Chain(v, dve_own)
            v.wait_ge(consts, 1)
            v.tensor_copy(m.identb[:, :], m.ident[:, :])
            v.tensor_copy(m.iota[:, :], iotai)
            v.wait_ge(ids_in, 6 * 16)
            v.tensor_copy(idf[:, :, :], ids[:, :, :]).then_inc(idf_ready, 1)
            v.wait_ge(id_ps, 1)
            pid = ps[:, 0, 0:3 * P].rearrange("p (w t) -> p w t", w=3)[:, :, 0:TILES]
            v.tensor_copy(m.srcf[:, :], pid[:, 0, :])
            v.tensor_copy(m.numbers[:, :, :].rearrange("p t w -> p w t"), pid)
            v.tensor_copy(idc[:, 0:3, :], pid)
            chain(v.tensor_copy(idi[:, 0:3, :], pid))
            for w in range(2):
                v.tensor_scalar(idi[:, 3 + w, :], idi[:, w, :], 8, None, ALU.arith_shift_right)
                chain(v.tensor_scalar(idi[:, w, :], idi[:, w, :], LO - 1, None, ALU.bitwise_and))
                v.tensor_copy(m.hl[:, 2 * w, :], idi[:, 3 + w, :])
                v.tensor_copy(m.hl[:, 2 * w + 1, :], idi[:, w, :])
                v.scalar_tensor_tensor(m.gidx[:, w, :], idc[:, w, :], float(N), idc[:, w, :], ALU.is_lt, ALU.mult)
            v.tensor_copy(m.gidx[:, 2, :], idc[:, 2, :])
            v.wait_ge(w_in, 6 * 16)
            for l in range(L):
                v.tensor_sub(raw[:, 1, l, :, :], raw[:, 1, l, :, :], raw[:, 0, l, :, :]).then_inc(wd_ready, 1)
            v.wait_ge(c_in, 32 * 16)
            for a, b in sorted(NEG):
                s = 64 * (a % 2)
                blk = cliff[s:s + 64, :, a // 2, 64 * b:64 * b + 64]
                last = v.tensor_scalar(blk, blk, -1.0, None, ALU.mult)
            last.then_inc(cl_ready, 1)
            for n in range(2 * L):
                v.wait_ge(w_ps, n + 1)
                l, w = n // 2, n % 2
                v.tensor_copy(m.wt[:, l, w, :, :], ps[:, 2 + n % 2, :].rearrange("p (h k) -> p h k", h=2)).then_inc(w_used, 1)
            v.wait_ge(cl_ps, 1)
            v.tensor_copy(m.upd[:, :, :].rearrange("p h (c b) -> p h b c", b=4),
                          ps[:, 4, :].rearrange("p (h b c) -> p h b c", h=2, b=4)).then_inc(kup_ready, 1)
            v.wait_ge(b_in, 17 * 16)
            v.tensor_copy(m.updb[:, :].rearrange("p (c b) -> p b c", b=4), rowb[:, 2, :].rearrange("p (b c) -> p b c", b=4))
            v.tensor_copy(rowb[:, 1, :].rearrange("p (b c) -> p b c", b=4), rowb[:, 0, :].rearrange("p (c b) -> p b c", b=4))
            for h in range(2):
                last = v.tensor_scalar(bcols[:, h, :], m.ones[:, :], bcol[:, h:h + 1], None, ALU.mult)
            last.then_inc(bc_ready, 1)
            v.wait_ge(bc_ready, 1)
            v.wait_ge(r_in, 16)
            for t in range(4):
                chain(v.scalar_tensor_tensor(rowb[0:RT, 3, :], relr[0:RT, t, 0:D], 1.0, rowb[0:RT, 1, :], ALU.mult, ALU.mult,
                                             accum_out=gz[0:RT, 1 + t:2 + t]))
            v.engine_nop().then_inc(gate_z, 1)
            v.wait_ge(msg_ps, 1)
            v.tensor_copy(m.msg[:, :, :], ps[:, 5, :].rearrange("p (h k) -> p h k", h=2))
            chain(v.tensor_copy(m.msgb[:, :], ps[:, 6, 0:D]))

        @block.scalar
        def _(a):
            a.wait_ge(gate_z, 1)
            a.activation(relr[0:RT, :, D], gz[0:RT, 1:5], ACT.Sigmoid, bias=gz[0:RT, 0:1]).then_inc(gate_s, 1)

        @block.tensor
        def _(pe):
            pe.wait_ge(idf_ready, 1)
            for w in range(3):
                last = pe.transpose(ps[:, 0, w * P:w * P + TILES], idf[:, w, :], m.ident[0:TILES, 0:TILES])
            last.then_inc(id_ps, 1)
            pe.wait_ge(wd_ready, L)
            for n in range(2 * L):
                l, w = n // 2, n % 2
                if n >= 2:
                    pe.wait_ge(w_used, n - 1)
                for kh in range(2):
                    for oh in range(2):
                        last = pe.transpose(ps[:, 2 + n % 2, kh * D + oh * P:kh * D + oh * P + P],
                                            raw[:, w, l, oh, kh * P:kh * P + P], m.ident[:, :])
                last.then_inc(w_ps, 1)
            pe.wait_ge(cl_ready, 1)
            for kh in range(2):
                for oh in range(2):
                    last = pe.transpose(ps[:, 4, kh * D + oh * P:kh * D + oh * P + P],
                                        cliff[:, 1, oh, kh * P:kh * P + P], m.ident[:, :])
            last.then_inc(cl_ps, 1)
            pe.wait_ge(kup_ready, 1)
            pe.wait_ge(bc_ready, 1)
            for kh in range(2):
                for mh in range(2):
                    pe.matmul(ps[:, 5, kh * D:kh * D + D], cliff[:, 0, mh, kh * P:kh * P + P], m.upd[:, mh, :],
                              start=(mh == 0), stop=(mh == 1))
            for mh in range(2):
                last = pe.matmul(ps[:, 6, 0:D], bcols[:, mh, :], m.upd[:, mh, :], start=(mh == 0), stop=(mh == 1))
            last.then_inc(msg_ps, 1)


def count_nodes(nc, m):
    sb, sem, ps = m.sb, m.sem, m.psum
    m.hot = m.big[:, 0:TILES * 2 * LO // 2].bitcast(BF16).rearrange("p (t w k) -> p t w k", t=TILES, w=2)
    DS = 8
    hotd = sb("hotd", [P, DS, 2, LO], BF16)
    cntf = sb("cntf", [P, 2, 2, LO], F32)
    incl = sb("incl", [P, 2, LO], F32)
    basef = sb("basef", [P, 2, LO], F32)
    off = sb("off", [P, 2], F32)
    tmp = sb("tmp1", [P, 2, LO], F32)
    table = sb("table", [P, 2, LO, 2], I32)
    hots_used = Signal(sem("hots_used"), DS - 1)
    hots_ready, cnt_ps, tot_ready, off_ps, table_ready, table_out = (
        sem(n) for n in ("hots_ready", "cnt_ps", "tot_ready", "off_ps", "table_ready", "table_out"))
    dve_own = sem("dve_own1")

    with nc.Block() as block:
        @block.vector
        def _(v):
            def hots(t, q, turn):
                hot = m.hot[:, bass.ds(t, 1), :, :].rearrange("p a w k -> p (a w) k")
                for w in range(2):
                    v.tensor_scalar(hot[:, w, :], m.iota[:, :], m.hl[:, w, bass.ds(t, 1)], None, ALU.is_equal)
                v.wait_ge(hots_used.sem, hots_used.free(t, DS))
                settle(v, m)
                for w in range(2):
                    last = v.tensor_scalar(hotd[:, q, w, :], m.iota[:, :], m.hl[:, 2 + w, bass.ds(t, 1)], None, ALU.is_equal)
                last.then_inc(hots_ready, 1)

            staged(v, TILES, DS, (0, hots))
            chain = Chain(v, dve_own)
            v.wait_ge(cnt_ps, 1)
            chain(v.tensor_copy(cntf[:, :, :, :], ps[:, 0:4, 0:LO].rearrange("p (w h) k -> p w h k", w=2)))
            chain(v.tensor_copy(m.cnt[:, 0, :, :], cntf[:, 0, :, :]))
            v.tensor_sub(m.cnt[:, 1, :, :], cntf[:, 0, :, :], m.cnt[:, 0, :, :])
            v.memset(basef[:, :, :], 0.0)
            v.memset(tmp[:, :, :], 1.0).then_inc(dve_own, 1)
            chain.k += 1
            v.wait_ge(dve_own, chain.k)
            for h in range(2):
                last = v.tensor_tensor_scan(incl[:, h, :], tmp[:, h, :], cntf[:, 0, h, :], 0.0, ALU.mult, ALU.add)
            last.then_inc(tot_ready, 1)
            v.wait_ge(off_ps, 1)
            chain(v.tensor_copy(off[:, :], ps[:, 4, 0:2]))
            for h in range(2):
                last = v.scalar_tensor_tensor(basef[:, h, :], incl[:, h, :], off[:, h:h + 1], cntf[:, 0, h, :], ALU.add, ALU.subtract)
            chain(last)
            chain(v.tensor_copy(m.base[:, 0, :, :], basef[:, :, :]))
            v.tensor_sub(m.base[:, 1, :, :], basef[:, :, :], m.base[:, 0, :, :])
            chain(v.scalar_tensor_tensor(tmp[:, :, :], basef[:, :, :], -1.0 - CROW, cntf[:, 0, :, :], ALU.add, ALU.add))
            chain(v.scalar_tensor_tensor(tmp[:, :, :], cntf[:, 0, :, :], 0.0, tmp[:, :, :], ALU.is_gt, ALU.mult))
            v.tensor_scalar(table[:, :, :, 0], tmp[:, :, :], float(CROW), None, ALU.add)
            v.tensor_copy(table[:, :, :, 1], cntf[:, 1, :, :]).then_inc(table_ready, 1)

        @block.tensor
        def _(pe):
            pe.sem_inc(hots_used.sem, hots_used.ahead)

            for n in range(4):
                pe.matmul(ps[:, n, 0:LO], m.zerob[:, 0:P], m.zerob[:, :], start=True, stop=True)

            def count(t, q, turn):
                pe.wait_ge(hots_ready, t + 1)
                hot = m.hot[:, bass.ds(t, 1), :, :].rearrange("p a w k -> p (a w) k")
                for h in range(2):
                    pe.matmul(ps[:, h, 0:LO], hot[:, 0, h * P:h * P + P], hot[:, 1, :], start=False, stop=True, skip_group_check=True)
                for h in range(2):
                    last = pe.matmul(ps[:, 2 + h, 0:LO], hotd[:, q, 0, h * P:h * P + P], hotd[:, q, 1, :], start=False, stop=True,
                                     skip_group_check=True)
                last.then_inc(hots_used.sem, 1)

            staged(pe, TILES, DS, (0, count))
            pe.matmul(ps[:, 5, 0:1], m.ones[:, :], m.ones[:, 0:1], start=True, stop=True).then_inc(cnt_ps, 1)
            pe.wait_ge(tot_ready, 1)
            pe.matmul(ps[:, 4, 0:2], m.before[:, :], incl[:, :, LO - 1], start=True, stop=False)
            pe.matmul(ps[:, 4, 1:2], m.ones[:, :], incl[:, 0, LO - 1:LO], start=False, stop=True).then_inc(off_ps, 1)

        @block.sync
        def _(sp):
            sp.wait_ge(table_ready, 1)
            for h in range(2):
                sp.dma_start(m.node_table.rearrange("(h p k) w -> h p (k w)", h=2, p=P)[h],
                             table[:, h, :, :].rearrange("p k w -> p (k w)")).then_inc(table_out, 16)
            sp.wait_ge(table_out, 32)


def rank_and_layer0(nc, m):
    sb, sem, ps = m.sb, m.sem, m.psum
    SLOTS = 4
    TS = 2 * SLOTS
    row = [sb(f"row{j}", [P, SW], F32) for j in range(TS)]
    xd = [sb(f"xd{j}", [P, D], F32) for j in range(TS)]
    gi = [sb(f"gi{j}", [P, 2], I32) for j in range(TS)]
    place = [sb(f"place{j}", [P, 1], I32) for j in range(TS)]
    stats = sb("stats", [P, 4, 6], F32)
    mv = sb("mv", [P, 4, 2], F32)
    std = sb("std", [P, 4], F32)
    rstd = sb("rstd", [P, 4], F32)
    nmr = sb("nmr", [P, 4], F32)
    h = sb("h", [P, 4, D], F32)
    hT = sb("hT", [P, 4, CW], F32)
    hotT = sb("hotT", [P, 4, P], BF16)
    run = sb("run", [P, 2, 2, LO], BF16)
    junk = m.meta[:, :, :].rearrange("p t w -> p (t w)")[:, 0:3 * CW].bitcast(BF16).rearrange("p (n k) -> p n k", n=6)
    keys = sb("keys_of_chunk", [P, 2, CW], I32)
    occ = sb("occ", [P, 2], F32)
    looked = sb("looked", [P, 2], F32)
    rankf = sb("rankf", [P, 2], F32)
    gathered = [sem(f"gathered{q}") for q in range(SLOTS)]
    scattered = [sem(f"scattered{q}") for q in range(SLOTS)]
    keys_in = [sem(f"keys_in{q}") for q in range(SLOTS)]
    (idx_ready, mv_ready, std_ready, ln_ready, h_ready, hT_ps, hT_ready, e_ready, hotT_ps, hotT_ready, looked_up,
     sel_done, run_ps, run_ready, row_ready, high_kept, rank_ready, dve_own) = (sem(n) for n in (
         "idx_ready", "mv_ready", "std_ready", "ln_ready", "h_ready", "hT_ps", "hT_ready", "e_ready", "hotT_ps",
         "hotT_ready", "looked_up", "sel_done", "run_ps", "run_ready", "row_ready", "high_kept", "rank_ready", "dve_own2"))
    occ_done = Signal(sem("occ_done"), 1)

    with nc.Block() as block:
        @block.sync
        def _(sp):
            def load_keys(c, q, turn):
                sp.wait_ge(occ_done.sem, occ_done.free(c, 2))
                sp.dma_start(keys[:, q % 2, :], bass.AP(tensor=m.keys.tensor, offset=c * CW, ap=[[0, P], [1, CW]]))\
                  .then_inc(keys_in[q], 16)

            staged(sp, CHUNKS, SLOTS, (0, load_keys))

        @block.gpsimd
        def _(g):
            for j in range(TS):
                g.memset(row[j][:, C_META:SW], 0.0)

            def gather(c, q, turn):
                g.wait_ge(scattered[q], turn * 32)
                for u in range(2):
                    last = g.tensor_copy(gi[2 * q + u][:, :], m.gidx[:, 0:2, bass.ds(c * 2 + u, 1)].rearrange("p w a -> p (w a)"))
                last.then_inc(idx_ready, 1)
                g.wait_ge(idx_ready, c + 1)
                settle(g, m)
                for j in (2 * q, 2 * q + 1):
                    for w, to in enumerate((row[j][:, C_X:C_X + D], xd[j][:, :])):
                        g.indirect_dma_start(out=to, out_offset=None, in_=m.x,
                                             in_offset=bass.IndirectOffsetOnAxis(ap=gi[j][:, w:w + 1], axis=0)).then_inc(gathered[q], 16)

            def scatter(c, q, turn):
                g.wait_ge(row_ready, c * 2 + 2)
                settle(g, m)
                for j in (2 * q, 2 * q + 1):
                    g.indirect_dma_start(out=m.sorted, out_offset=bass.IndirectOffsetOnAxis(ap=place[j][:, 0:1], axis=0),
                                         in_=row[j][:, :], in_offset=None).then_inc(scattered[q], 16)

            staged(g, CHUNKS, SLOTS, (0, scatter), (3, gather))
            for q in range(SLOTS):
                g.wait_ge(scattered[q], len(range(q, CHUNKS, SLOTS)) * 32)

        @block.vector
        def _(v):
            chain = Chain(v, dve_own)
            v.sem_inc(occ_done.sem, occ_done.ahead)
            v.tensor_copy(run[:, :, :, :], m.base[:, :, :, :]).then_inc(run_ready, 1)

            def statistics(c, q, turn):
                slots = (2 * q, 2 * q + 1)
                v.wait_ge(gathered[q], (turn + 1) * 4 * 16)
                for u, j in enumerate(slots):
                    v.bn_stats(stats[:, u, :], xd[j][:, :])
                    last = v.bn_stats(stats[:, 2 + u, :], row[j][:, C_X:C_X + D])
                chain(last)
                settle(v, m)
                for n in range(4):
                    last = v.bn_aggr(mv[:, n, :], stats[:, n, :])
                last.then_inc(mv_ready, 1)

            def scales(c, q, turn):
                v.wait_ge(std_ready, c + 1)
                v.wait_ge(h_ready, c)
                chain(v.reciprocal(rstd[:, :], std[:, :]))
                v.scalar_tensor_tensor(nmr[:, :], mv[:, :, 0], -1.0, rstd[:, :], ALU.mult, ALU.mult).then_inc(ln_ready, 1)

            def count_equal(c, q, turn):
                v.wait_ge(keys_in[q], (turn + 1) * 16)
                for u in range(2):
                    last = v.scalar_tensor_tensor(junk[:, u, :], keys[:, q % 2, :], m.srcf[:, bass.ds(c * 2 + u, 1)],
                                                  m.earlier[:, u, :], ALU.is_equal, ALU.mult, accum_out=occ[:, u:u + 1])
                last.then_inc(occ_done.sem, 1)

            def place_edges(c, q, turn):
                slots = (2 * q, 2 * q + 1)
                v.wait_ge(looked_up, c + 1)
                for u in range(2):
                    hot = m.hot[:, bass.ds(c * 2 + u, 1), 1, :].rearrange("p a k -> p (a k)")
                    v.scalar_tensor_tensor(junk[:, 2 + u, :], ps[:, 4, u * LO:u * LO + LO], 1.0, hot, ALU.mult, ALU.mult,
                                           accum_out=looked[:, u:u + 1])
                    last = v.scalar_tensor_tensor(junk[:, 4 + u, :], ps[:, 5, u * LO:u * LO + LO], 1.0, hot, ALU.mult, ALU.mult,
                                                  accum_out=row[2 * q + u][:, C_META + M_SCALE:C_META + M_SCALE + 1])
                last.then_inc(sel_done, 1)
                v.wait_ge(run_ps, c + 1)
                v.tensor_copy(run[:, 0, :, :], ps[:, 6:8, 0:LO]).then_inc(high_kept, 1)
                v.wait_ge(sel_done, c + 1)
                v.wait_ge(occ_done.sem, occ_done.done(c))
                v.tensor_tensor(rankf[:, :], looked[:, :], occ[:, :], ALU.add).then_inc(rank_ready, 1)
                v.wait_ge(high_kept, c + 1)
                v.tensor_sub(run[:, 1, :, :], ps[:, 6:8, 0:LO], run[:, 0, :, :]).then_inc(run_ready, 1)
                v.wait_ge(rank_ready, c + 1)
                settle(v, m)
                for u, j in enumerate(slots):
                    v.tensor_copy(place[j][:, :], rankf[:, u:u + 1])
                    v.tensor_copy(row[j][:, C_META + M_SRC:C_META + M_TYPE + 1],
                                  m.numbers[:, bass.ds(c * 2 + u, 1), :].rearrange("p a w -> p (a w)"))

            def finish(c, q, turn):
                v.wait_ge(e_ready, c + 1)
                for u in range(2):
                    v.tensor_scalar(row[2 * q + u][:, C_E:C_E + D], ps[:, 2, u * D:u * D + D], 0.0, None, ALU.max).then_inc(row_ready, 1)

            staged(v, CHUNKS, SLOTS, (0, finish), (1, count_equal), (2, statistics), (2, scales), (1, place_edges),
                   chain=chain, counts=(0, 0, 1, 1, 0))

        @block.scalar
        def _(a):
            def one_hots(c, q, turn):
                a.wait_ge(hotT_ps, c + 1)
                a.wait_ge(looked_up, c)
                a.activation(hotT[:, :, :].rearrange("p a k -> p (a k)"), ps[:, 3, :], ACT.Copy).then_inc(hotT_ready, 1)

            def normalise(c, q, turn):
                a.wait_ge(ln_ready, c + 1)
                a.wait_ge(hT_ps, c)
                for u in range(2):
                    j = 2 * q + u
                    a.activation(h[:, u, :], xd[j][:, :], ACT.Relu, bias=nmr[:, u:u + 1], scale=rstd[:, u:u + 1])
                    last = a.activation(h[:, 2 + u, :], row[j][:, C_X:C_X + D], ACT.Relu,
                                        bias=nmr[:, 2 + u:3 + u], scale=rstd[:, 2 + u:3 + u])
                last.then_inc(h_ready, 1)

            def transposed(c, q, turn):
                a.wait_ge(hT_ps, c + 1)
                a.wait_ge(e_ready, c)
                for s in range(2):
                    last = a.activation(hT[:, 2 * s:2 * s + 2, :].rearrange("p a k -> p (a k)"), ps[:, s, :], ACT.Copy)
                last.then_inc(hT_ready, 1)

            def root_of_variance(c, q, turn):
                a.wait_ge(mv_ready, c + 1)
                a.activation(std[:, :], mv[:, :, 1], ACT.Sqrt, bias=m.eps[:, :]).then_inc(std_ready, 1)

            staged(a, CHUNKS, SLOTS, (1, transposed), (2, root_of_variance), (2, normalise), (2, one_hots))

        @block.tensor
        def _(pe):
            for hh in range(2):
                for part in range(2):
                    pe.matmul(ps[:, 6 + hh, 0:LO], m.identb[:, :], m.base[:, part, hh, :], start=(part == 0), stop=(part == 1))

            def turn_one_hots(c, q, turn):
                hot = m.hot[:, bass.ds(c * 2, 2), :, :]
                for n in range(4):
                    last = pe.matmul(ps[:, 3, n * P:n * P + P], hot[:, n // 2, 0, (n % 2) * P:(n % 2) * P + P],
                                     m.identb[:, :], start=True, stop=True)
                last.then_inc(hotT_ps, 1)

            def rank(c, q, turn):
                hot = m.hot[:, bass.ds(c * 2, 2), :, :]
                pe.wait_ge(hotT_ready, c + 1)
                pe.wait_ge(run_ready, c + 1)
                pe.wait_ge(sel_done, c)
                for u in range(2):
                    for n in range(4):
                        pe.matmul(ps[:, 4, u * LO:u * LO + LO], hotT[:, 2 * u + n % 2, :], run[:, n // 2, n % 2, :],
                                  start=(n == 0), stop=(n == 3))
                    for n in range(4):
                        last = pe.matmul(ps[:, 5, u * LO:u * LO + LO], hotT[:, 2 * u + n % 2, :], m.cnt[:, n // 2, n % 2, :],
                                         start=(n == 0), stop=(n == 3))
                last.then_inc(looked_up, 1)
                for n in range(4):
                    u, hh = n // 2, n % 2
                    last = pe.matmul(ps[:, 6 + hh, 0:LO], hot[:, u, 0, hh * P:hh * P + P], hot[:, u, 1, :], start=False, stop=True,
                                     skip_group_check=True)
                last.then_inc(run_ps, 1)

            def turn_features(c, q, turn):
                pe.wait_ge(h_ready, c + 1)
                for n in range(8):
                    side, u, kh = n // 4, n // 2 % 2, n % 2
                    last = pe.transpose(ps[:, side, kh * CW + u * P:kh * CW + u * P + P],
                                        h[:, 2 * side + u, kh * P:kh * P + P], m.ident[:, :])
                last.then_inc(hT_ps, 1)

            def values(c, q, turn):
                pe.wait_ge(hT_ready, c + 1)
                pe.wait_ge(row_ready, c * 2)
                for u in range(2):
                    for n in range(4):
                        last = pe.matmul(ps[:, 2, u * D:u * D + D], hT[:, n, u * P:u * P + P], m.wt[:, 0, n // 2, n % 2, :],
                                         start=(n == 0), stop=(n == 3))
                last.then_inc(e_ready, 1)

            staged(pe, CHUNKS, SLOTS, (0, values), (1, turn_features), (1, rank), (2, turn_one_hots))


def scan_forward(nc, m, l):
    sb, ps = m.sb, m.psum
    sem = lambda n: m.sem(f"{n}_f{l}")
    SLOTS = 4
    rows = sb("rows", [P, 2 * SLOTS, D], F32)
    masked = sb("masked", [P, 2, 2, CW], F32)
    junk = sb("junk_f", [P, 2, 2, CW], BF16)
    t2 = sb("t2", [P, 8, 2], F32)
    loaded = [sem(f"loaded{q}") for q in range(SLOTS)]
    meta_in, diag_ready, pi_ready, flags_ready, dve_own = (
        sem(n) for n in ("meta_in", "diag_ready", "pi_ready", "flags_ready", "dve_own"))
    masked_ready, var_ready, std_ready = (sem(n) for n in ("masked_ready", "var_ready", "std_ready"))
    val_ps = Signal(sem("val_ps"), SLOTS - 1)
    scanned = Signal(sem("scanned"), SLOTS - 1)
    values_used = scanned if l == 0 else Signal(sem("values_used"), SLOTS - 1)
    squared = Signal(sem("squared"), 1)
    keys_ps, same_ready = Signal(sem("keys_ps"), SLOTS - 1), Signal(sem("same_ready"), 1)
    if l == 0:
        diag = sb("diag", [P, SLOTS, 2, P], F32)
        krow = sb("krow", [P, 2, 1 + CW], F32)
        node = sb("node", [P, SLOTS, 2], I32)
        found = [sb(f"found{j}", [P, 2], I32) for j in range(2 * SLOTS)]
        degrees = sb("degrees", [P, 2, TILES], F32)
        looked_up = [sem(f"looked_up{q}") for q in range(SLOTS)]
        kept, degrees_ready, root_ready = (sem(n) for n in ("kept", "degrees_ready", "root_ready"))
    else:
        turned = sb("turned", [P, 2, 2 * CW], F32)
        summed = sb("summed", [P, 2, 2 * CW], F32)
        turned_ready = sem("turned_ready")
        pidx = sb("pidx", [P, SLOTS, 2], I32)

    with nc.Block() as block:
        @block.sync
        def _(sp):
            def load(c, q, turn):
                sp.wait_ge(val_ps.sem, val_ps.free(c, SLOTS))
                sp.dma_start(rows[:, 2 * q:2 * q + 2, :],
                             m.sorted[bass.ds(c * CW, CW), C_E:C_E + D].rearrange("(u p) k -> p u k", p=P)).then_inc(loaded[q], 16)

            if l == 0:
                sp.dma_start(m.meta[:, :, :], m.sorted.rearrange("(t p) w -> p t w", p=P)[:, :, C_META:SW]).then_inc(meta_in, 16)
                staged(sp, CHUNKS, SLOTS, (0, load))

        @block.gpsimd
        def _(g):
            def find(c, q, turn):
                g.wait_ge(val_ps.sem, val_ps.free(c, SLOTS))
                settle(g, m)
                g.tensor_copy(pidx[:, q, :], m.meta[:, bass.ds(c * 2, 2), M_POS].bitcast(I32)).then_inc(pi_ready, 1)

            def gather(c, q, turn):
                g.wait_ge(pi_ready, c + 1)
                g.wait_ge(val_ps.sem, val_ps.free(c, SLOTS))
                settle(g, m)
                for u in range(2):
                    g.indirect_dma_start(out=rows[:, 2 * q + u, :], out_offset=None, in_=m.projected,
                                         in_offset=bass.IndirectOffsetOnAxis(ap=pidx[:, q, u:u + 1], axis=0)).then_inc(loaded[q], 16)

            def look_up(c, q, turn):
                g.tensor_copy(node[:, q, :], m.meta[:, bass.ds(c * 2, 2), M_DST]).then_inc(pi_ready, 1)
                g.wait_ge(pi_ready, c + 1)
                settle(g, m)
                for u in range(2):
                    g.indirect_dma_start(out=found[2 * q + u][:, :], out_offset=None, in_=m.node_table,
                                         in_offset=bass.IndirectOffsetOnAxis(ap=node[:, q, u:u + 1], axis=0)).then_inc(looked_up[q], 16)

            def keep(c, q, turn):
                g.wait_ge(looked_up[q], (turn + 1) * 32)
                settle(g, m)
                for u in range(2):
                    last = g.tensor_copy(m.meta[:, bass.ds(c * 2 + u, 1), M_POS:M_IN + 1].rearrange("p a w -> p (a w)").bitcast(I32),
                                         found[2 * q + u][:, :])
                last.then_inc(kept, 1)

            if l > 0:
                staged(g, CHUNKS, SLOTS, (1, find), (0, gather))
            else:
                g.wait_ge(meta_in, 16)
                staged(g, CHUNKS, SLOTS, (2, look_up), (0, keep))

        @block.scalar
        def _(a):
            a.sem_inc(squared.sem, squared.ahead)

            def key_diagonals(c, q, turn):
                a.wait_ge(keys_ps.sem, keys_ps.free(c, SLOTS))
                for u in range(2):
                    last = a.activation(diag[:, q, u, :], m.ident[:, :], ACT.Copy, scale=m.meta[:, bass.ds(c * 2 + u, 1), M_SRC])
                last.then_inc(diag_ready, 1)

            def copy_gathered(c, q, turn):
                a.wait_ge(val_ps.sem, val_ps.done(c))
                a.wait_ge(values_used.sem, values_used.free(c, 2))
                a.activation(turned[:, q % 2, :], ps[:, SLOTS + q, :], ACT.Copy).then_inc(turned_ready, 1)

            def squares(c, q, turn):
                a.wait_ge(masked_ready, c + 1)
                for h in range(2):
                    last = a.activation(junk[:, q % 2, h, :], masked[:, q % 2, h, :], ACT.Square,
                                        accum_out=m.sums[:, 1, h, bass.ds(c, 1)])
                last.then_inc(squared.sem, 1)

            if l == 0:
                a.wait_ge(meta_in, 16)
            if l == 0:
                staged(a, CHUNKS, SLOTS, (5, key_diagonals), (0, squares))
            else:
                staged(a, CHUNKS, SLOTS, (2, copy_gathered), (0, squares))
            a.wait_ge(var_ready, 1)
            a.activation(t2[:, 4, :], t2[:, 3, :], ACT.Sqrt, bias=m.eps[:, :]).then_inc(std_ready, 1)
            if l == 0:
                a.wait_ge(degrees_ready, 1)
                a.activation(degrees[:, 1, :], degrees[:, 0, :], ACT.Sqrt).then_inc(root_ready, 1)

        @block.tensor
        def _(pe):
            pe.sem_inc(val_ps.sem, val_ps.ahead)
            pe.sem_inc(keys_ps.sem, keys_ps.ahead)

            def key_rows(c, q, turn):
                pe.wait_ge(diag_ready, c + 1)
                pe.wait_ge(same_ready.sem, same_ready.free(c, 2))
                pe.matmul(ps[:, 4 + q % 2, 0:CW], m.ones[:, :], diag[:, q, :, :].rearrange("p u k -> p (u k)"),
                          start=True, stop=True).then_inc(keys_ps.sem, 1)

            def values(c, q, turn):
                pe.wait_ge(loaded[q], (turn + 1) * (16 if l == 0 else 32))
                pe.wait_ge(values_used.sem, values_used.free(c, SLOTS))
                for h in range(2):
                    o = ps[:, q, h * CW:h * CW + CW]
                    for u in range(2):
                        data = rows[:, 2 * q + u, h * P:h * P + P]
                        if l == 0:
                            last = pe.transpose(o[:, u * P:u * P + P], data, m.ident[:, :])
                        else:
                            for kh in range(2):
                                pe.matmul(o[:, u * P:u * P + P], m.wt[:, l, 1, kh, h * P:h * P + P],
                                          m.feat[:, kh, bass.ds(c * CW + (1 + u * P), P)], start=(kh == 0), stop=(kh == 1))
                            last = pe.transpose(ps[:, SLOTS + q, h * CW + u * P:h * CW + u * P + P], data, m.ident[:, :])
                last.then_inc(val_ps.sem, 1)

            if l == 0:
                staged(pe, CHUNKS, SLOTS, (2, key_rows), (0, values))
            else:
                staged(pe, CHUNKS, SLOTS, (0, values))

        @block.vector
        def _(v):
            chain = Chain(v, dve_own)
            v.sem_inc(scanned.sem, scanned.ahead)
            if l > 0:
                v.sem_inc(values_used.sem, values_used.ahead)
            v.sem_inc(same_ready.sem, same_ready.ahead)
            if l == 0:
                v.memset(m.feat[:, :, 0:1], 0.0)
                v.memset(m.feat[:, :, EP + 1:EP + 2], 0.0)
                v.memset(m.same[:, EP:EP + 1], 0.0)
                chain(v.memset(krow[:, 1, CW:CW + 1], -1.0))

            def copy_keys(c, q, turn):
                q = q % 2
                v.wait_ge(keys_ps.sem, keys_ps.done(c))
                v.tensor_copy(krow[:, q, 0:1], krow[:, 1 - q, CW:CW + 1])
                v.tensor_copy(krow[:, q, 1:1 + CW], ps[:, 4 + q, 0:CW]).then_inc(same_ready.sem, 1)

            def run_flags(c, q, turn):
                q = q % 2
                v.wait_ge(same_ready.sem, same_ready.done(c))
                settle(v, m)
                v.tensor_tensor(m.same[:, bass.ds(c * CW, CW)], krow[:, q, 1:1 + CW], krow[:, q, 0:CW], ALU.is_equal).then_inc(flags_ready, 1)

            def scan(c, q, turn):
                same = m.same[:, bass.ds(c * CW, CW)]
                if l == 0:
                    v.wait_ge(flags_ready, c + 1)
                    settle(v, m)
                    v.wait_ge(val_ps.sem, val_ps.done(c))
                else:
                    v.wait_ge(values_used.sem, values_used.done(c))
                for h in range(2):
                    values = ps[:, q, h * CW:h * CW + CW] if l == 0 else summed[:, q % 2, h * CW:h * CW + CW]
                    last = v.tensor_tensor_scan(m.feat[:, h, bass.ds(c * CW + 1, CW)], same, values,
                                                m.feat[:, h, bass.ds(c * CW, 1)], ALU.mult, ALU.max)
                last.then_inc(scanned.sem, 1)

            def add_gathered(c, q, turn):
                v.wait_ge(turned_ready, c + 1)
                v.tensor_tensor(summed[:, q % 2, :], ps[:, q, :], turned[:, q % 2, :], ALU.add).then_inc(values_used.sem, 1)

            def add_up(c, q, turn):
                same = m.same[:, bass.ds(c * CW, CW)]
                v.wait_ge(scanned.sem, scanned.done(c))
                v.wait_ge(squared.sem, squared.free(c, 2))
                for h in range(2):
                    last = v.scalar_tensor_tensor(masked[:, q % 2, h, :], same, 0.0, m.feat[:, h, bass.ds(c * CW, CW)],
                                                  ALU.is_equal, ALU.mult, accum_out=m.sums[:, 0, h, bass.ds(c, 1)])
                last.then_inc(masked_ready, 1)

            if l == 0:
                staged(v, CHUNKS, SLOTS, (1, copy_keys), (0, scan), (1, run_flags), (0, add_up))
            else:
                staged(v, CHUNKS, SLOTS, (0, scan), (1, add_gathered), (0, add_up))
            v.wait_ge(masked_ready, CHUNKS)
            v.wait_ge(squared.sem, squared.done(CHUNKS - 1))
            chain(v.tensor_reduce(t2[:, 0:2, :].rearrange("p a b -> p (a b)"), m.sums[:, :, :, :].rearrange("p a h c -> p (a h) c"),
                                  mybir.AxisListType.X, ALU.add))
            chain(v.tensor_scalar(t2[:, 0:2, :], t2[:, 0:2, :], 1.0 / N, None, ALU.mult))
            chain(v.tensor_tensor(t2[:, 2, :], t2[:, 0, :], t2[:, 0, :], ALU.mult))
            v.tensor_tensor(t2[:, 3, :], t2[:, 1, :], t2[:, 2, :], ALU.subtract).then_inc(var_ready, 1)
            v.wait_ge(std_ready, 1)
            chain(v.reciprocal(t2[:, 5, :], t2[:, 4, :]))
            chain(v.tensor_tensor(m.coef[:, 0, :], t2[:, 5, :], m.gam[:, l, :], ALU.mult))
            chain(v.tensor_tensor(t2[:, 6, :], m.coef[:, 0, :], t2[:, 0, :], ALU.mult))
            chain(v.tensor_tensor(m.coef[:, 1, :], m.bet[:, l, :], t2[:, 6, :], ALU.subtract))
            chain(v.tensor_scalar(m.coef[:, 2, :], m.coef[:, 1, :], 0.0, None, ALU.max))
            if l == 0:
                v.wait_ge(kept, CHUNKS)
                chain(v.tensor_copy(degrees[:, 0, :], m.meta[:, :, M_IN].bitcast(I32)))
                chain(v.tensor_tensor(degrees[:, 0, :], degrees[:, 0, :], m.meta[:, :, M_SCALE], ALU.mult))
                v.tensor_scalar(degrees[:, 0, :], degrees[:, 0, :], 1.0, None, ALU.max).then_inc(degrees_ready, 1)
                v.wait_ge(root_ready, 1)
                chain(v.reciprocal(m.meta[:, :, M_SCALE], degrees[:, 1, :]))


class BackwardScan:

    def __init__(self, nc, m, sem, used):
        self.m, self.used = m, used
        self.vals = m.sb("back_vals", [P, 2, 2, CW], F32)
        self.same = m.sb("back_same", [P, 2, CW], BF16)
        self.carry = m.sb("back_carry", [P, 2, 2, 1], F32)
        self.filled, self.done = sem("back_filled"), sem("back_done")

    def init(self, v):
        v.memset(self.carry[:, 1, :, :], 0.0).then_inc(self.done, 1)

    def fill(self, v, j, q):
        v.wait_ge(self.used.sem, self.used.free(j, 2))
        settle(v, self.m)
        v.tensor_copy(self.same[:, q, :], self.m.same[:, bass.ds(from_end(j) * CW + 1, CW)])
        v.tensor_copy(self.vals[:, q, :, :], self.m.feat[:, :, bass.ds(from_end(j) * CW + 1, CW)]).then_inc(self.filled, 1)

    def scan(self, v, j, q):
        v.wait_ge(self.filled, j + 1)
        v.wait_ge(self.done, j * 2 + 1)
        for h in range(2):
            f = self.vals[:, q, h, ::-1]
            last = v.tensor_tensor_scan(f, self.same[:, q, ::-1], f, self.carry[:, 1 - q, h, :], ALU.mult, ALU.max)
        last.then_inc(self.done, 1)

    def keep_carry(self, v, j, q):
        v.wait_ge(self.done, j * 2 + 2)
        v.tensor_copy(self.carry[:, q, :, :], self.vals[:, q, :, 0:1]).then_inc(self.done, 1)

    def scanned(self, j):
        return j * 2 + 2


def from_end(j):
    return (CHUNKS - 1) - j


def project(nc, m, l):
    sb, ps = m.sb, m.psum
    sem = lambda n: m.sem(f"{n}_p{l}")
    xc = sb("xc_p", [P, 2, 2, CW], F32)
    crow = sb("crow", [P, 2, P], F32)
    rows = sb("rows_p", [P, 2, 2, D], F32)
    c_out = sb("c_out", [P, D], F32)
    c_ready, c_ps, cout_ready, cout_done = (sem(n) for n in ("c_ready", "c_ps", "cout_ready", "cout_done"))
    xc_ready, rows_ps, rows_ready, kept = (Signal(sem(n), 1) for n in ("xc_ready", "rows_ps", "rows_ready", "kept"))
    stored = [sem(f"stored{q}") for q in range(2)]
    back = BackwardScan(nc, m, sem, xc_ready)

    with nc.Block() as block:
        @block.vector
        def _(v):
            for h in range(2):
                last = v.tensor_scalar(crow[:, h, :], m.ones[:, :], m.coef[:, 2, h:h + 1], None, ALU.mult)
            last.then_inc(c_ready, 1)
            back.init(v)
            v.wait_ge(c_ps, 1)
            v.tensor_copy(c_out[:, :], ps[:, 4, 0:D]).then_inc(cout_ready, 1)

            def fill(j, q, turn):
                back.fill(v, j, q)

            def back_scan(j, q, turn):
                back.scan(v, j, q)

            def keep_carry(j, q, turn):
                back.keep_carry(v, j, q)

            staged(v, CHUNKS, 2, (0, back_scan), (1, fill), (0, keep_carry))
            if l == 1:
                v.wait_ge(rows_ps.sem, rows_ps.done(CHUNKS - 1))
                v.scalar_tensor_tensor(m.last_src[:, :], ps[:, 5, 0:TILES], float(2 * N), m.meta[:, :, M_SRC], ALU.mult, ALU.add)

        @block.gpsimd
        def _(g):
            g.sem_inc(kept.sem, kept.ahead)

            def keep(j, q, turn):
                g.wait_ge(xc_ready.sem, xc_ready.done(j))
                settle(g, m)
                g.tensor_copy(m.feat[:, :, bass.ds(from_end(j) * CW + 1, CW)], xc[:, q, :, :]).then_inc(kept.sem, 1)

            staged(g, CHUNKS, 2, (0, keep))

        @block.scalar
        def _(a):
            a.sem_inc(rows_ready.sem, rows_ready.ahead)
            a.sem_inc(xc_ready.sem, xc_ready.ahead)

            def features(j, q, turn):
                a.wait_ge(back.done, back.scanned(j))
                a.wait_ge(rows_ps.sem, rows_ps.free(j, 2))
                a.wait_ge(kept.sem, kept.free(j, 2))
                for h in range(2):
                    last = a.activation(xc[:, q, h, :], back.vals[:, q, h, :], ACT.Relu,
                                        bias=m.coef[:, 1, h:h + 1], scale=m.coef[:, 0, h:h + 1])
                last.then_inc(xc_ready.sem, 1)

            def copy_rows(j, q, turn):
                a.wait_ge(rows_ps.sem, rows_ps.done(j))
                a.wait_ge(stored[q], turn * 16)
                a.activation(rows[:, q, :, :].rearrange("p u k -> p (u k)"), ps[:, q, :], ACT.Copy).then_inc(rows_ready.sem, 1)

            staged(a, CHUNKS, 2, (1, features), (0, copy_rows))

        @block.tensor
        def _(pe):
            pe.sem_inc(rows_ps.sem, rows_ps.ahead)
            pe.wait_ge(c_ready, 1)
            for kh in range(2):
                last = pe.matmul(ps[:, 4, 0:D], crow[:, kh, :], m.wt[:, l, 0, kh, :], start=(kh == 0), stop=(kh == 1))
            last.then_inc(c_ps, 1)

            def products(j, q, turn):
                pe.wait_ge(xc_ready.sem, xc_ready.done(j))
                pe.wait_ge(rows_ready.sem, rows_ready.free(j, 2))
                settle(pe, m)
                if l == 1:
                    for u in range(2):
                        pe.matmul(ps[:, 5, bass.ds(from_end(j) * 2 + u, 1)], m.same[:, bass.ds(from_end(j) * CW + (u * P + 1), P)],
                                  m.identb[:, 0:1], start=True, stop=True)
                for u in range(2):
                    for kh in range(2):
                        last = pe.matmul(ps[:, q, u * D:u * D + D], xc[:, q, kh, u * P:u * P + P], m.wt[:, l, 0, kh, :],
                                         start=(kh == 0), stop=(kh == 1))
                last.then_inc(rows_ps.sem, 1)

            staged(pe, CHUNKS, 2, (0, products))

        @block.sync
        def _(sp):
            sp.wait_ge(cout_ready, 1)
            sp.dma_start(m.projected[CROW:CROW + P, :], c_out[:, :]).then_inc(cout_done, 16)

            def store(j, q, turn):
                sp.wait_ge(rows_ready.sem, rows_ready.done(j))
                settle(sp, m)
                sp.dma_start(m.projected[bass.ds(from_end(j) * CW, CW), :].rearrange("(u p) k -> p u k", p=P),
                             rows[:, q, :, :]).then_inc(stored[q], 16)

            staged(sp, CHUNKS, 2, (0, store))
            sp.wait_ge(cout_done, 16)
            for q in range(2):
                sp.wait_ge(stored[q], CHUNKS // 2 * 16)


def messages(nc, m):
    sb, ps = m.sb, m.psum
    sem = lambda n: m.sem(f"{n}_m")
    xc = sb("xc_m", [P, 2, CW], F32)
    LD = 4
    ld = sb("ld", [P, LD, 2, 2 * D], F32)
    scales_ready = sem("scales_ready")
    used_up = m.wt.rearrange("p l s k o -> p (l s k o)")
    xp = used_up[:, 8 * CW:8 * CW + 4 * D].rearrange("p (q u k) -> p q u k", q=2, u=2)
    xb = sb("xb", [P, LD, 2, D], F32)
    hg = sb("hg", [P, 2, 2, 2, D], F32)
    hgT = used_up[:, 0:8 * CW].rearrange("p (q s k e) -> p q s k e", q=2, s=2, k=2)
    res = sb("res", [P, 2, 2, 2, D], F32)
    stats = sb("stats_m", [P, 2, 6], F32)
    mv = sb("mv_m", [P, 2, 2], F32)
    std = sb("std_m", [P, 2], F32)
    rstd = sb("rstd_m", [P, 2], F32)
    nmr = sb("nmr_m", [P, 2], F32)
    x_ps, xp_ready, mv_ready, std_ready, ln_ready, stats_ready, dve_own = (
        sem(n) for n in ("x_ps", "xp_ready", "mv_ready", "std_ready", "ln_ready", "stats_ready", "dve_own"))
    xc_ready, h_ready, xb_ready, hgT_ps, hgT_ready, out_ps, out_ready, y_ready = (
        Signal(sem(n), 1) for n in ("xc_ready", "h_ready", "xb_ready", "hgT_ps", "hgT_ready", "out_ps", "out_ready", "y_ready"))
    g_ready = Signal(sem("g_ready"), LD - 1)
    out_ready = Signal(out_ready.sem, LD - 1)
    loaded = [sem(f"loaded{q}") for q in range(LD)]
    stored = [sem(f"stored{q}") for q in range(2)]
    rewritten = [sem(f"rewritten{q}") for q in range(LD)]
    rewrite_to = sb("rewrite_to", [P, 2, 2], I32)
    back = BackwardScan(nc, m, sem, xc_ready)

    with nc.Block() as block:
        @block.sync
        def _(sp):
            def load(j, q, turn):
                sp.wait_ge(g_ready.sem, g_ready.free(j, LD))
                settle(sp, m)
                for w, rows in enumerate((m.sorted[bass.ds(from_end(j) * CW, CW), C_X:C_X + D],
                                          m.relations[bass.ds(from_end(j) * CW, CW), :])):
                    sp.dma_start(ld[:, q, :, w * D:w * D + D], rows.rearrange("(u p) w -> p u w", p=P)).then_inc(loaded[q], 16)

            def store(j, q, turn):
                sp.wait_ge(y_ready.sem, y_ready.done(j))
                settle(sp, m)
                sp.dma_start(m.messages[bass.ds(from_end(j) * CW, CW), :].rearrange("(u p) k -> p u k", p=P),
                             res[:, q % 2, 1, :, :]).then_inc(stored[q % 2], 16)

            staged(sp, CHUNKS, LD, (5, load), (0, store))
            for q in range(2):
                sp.wait_ge(stored[q], CHUNKS // 2 * 16)

        @block.gpsimd
        def _(g):
            g.sem_inc(g_ready.sem, g_ready.ahead)
            g.sem_inc(xb_ready.sem, xb_ready.ahead)

            def times_relation(j, q, turn):
                g.wait_ge(h_ready.sem, h_ready.done(j))
                g.wait_ge(hgT_ps.sem, hgT_ps.free(j, 2))
                g.tensor_tensor(hg[:, q % 2, 1, :, :], hg[:, q % 2, 0, :, :], ld[:, q, :, D:2 * D], ALU.mult).then_inc(g_ready.sem, 1)

            def plus_bias(j, q, turn):
                g.wait_ge(xp_ready, j + 1)
                g.wait_ge(out_ready.sem, out_ready.free(j, LD))
                for u in range(2):
                    last = g.tensor_tensor(xb[:, q, u, :], xp[:, q % 2, u, :], m.updb[:, :], ALU.add)
                last.then_inc(xb_ready.sem, 1)

            def rewrite(j, q, turn):
                g.wait_ge(out_ready.sem, out_ready.done(j))
                settle(g, m)
                for u in range(2):
                    g.indirect_dma_start(out=m.out, out_offset=bass.IndirectOffsetOnAxis(ap=rewrite_to[:, q % 2, u:u + 1], axis=0),
                                         in_=res[:, q % 2, 0, u, :], in_offset=None,
                                         bounds_check=N - 1, oob_is_err=False).then_inc(rewritten[q], 16)

            staged(g, CHUNKS, LD, (3, plus_bias), (3, times_relation), (0, rewrite))
            for q in range(LD):
                g.wait_ge(rewritten[q], len(range(q, CHUNKS, LD)) * 32)

        @block.scalar
        def _(a):
            a.sem_inc(h_ready.sem, h_ready.ahead)
            a.sem_inc(xc_ready.sem, xc_ready.ahead)
            a.sem_inc(hgT_ready.sem, hgT_ready.ahead)
            a.sem_inc(y_ready.sem, y_ready.ahead)
            a.wait_ge(scales_ready, 1)

            def features(j, q, turn):
                a.wait_ge(back.done, back.scanned(j))
                a.wait_ge(x_ps, j)
                for h in range(2):
                    last = a.activation(xc[:, h, :], back.vals[:, q, h, :], ACT.Relu,
                                        bias=m.coef[:, 1, h:h + 1], scale=m.coef[:, 0, h:h + 1])
                last.then_inc(xc_ready.sem, 1)

            def normalise(j, q, turn):
                a.wait_ge(ln_ready, j + 1)
                a.wait_ge(hgT_ps.sem, hgT_ps.free(j, 2))
                for u in range(2):
                    last = a.activation(hg[:, q, 0, u, :], xp[:, q, u, :], ACT.Relu, bias=nmr[:, u:u + 1], scale=rstd[:, u:u + 1])
                last.then_inc(h_ready.sem, 1)

            def transposed(j, q, turn):
                a.wait_ge(hgT_ps.sem, hgT_ps.done(j))
                a.wait_ge(out_ps.sem, out_ps.free(j, 2))
                for s in range(2):
                    last = a.activation(hgT[:, q, s, :, :].rearrange("p k e -> p (k e)"), ps[:, 1 + s, :], ACT.Copy)
                last.then_inc(hgT_ready.sem, 1)

            def root(j, q, turn):
                a.wait_ge(mv_ready, j + 1)
                a.activation(std[:, :], mv[:, :, 1], ACT.Sqrt, bias=m.eps[:, :]).then_inc(std_ready, 1)

            def scale(j, q, turn):
                a.wait_ge(out_ready.sem, out_ready.done(j))
                for u in range(2):
                    y = res[:, q, 1, u, :]
                    last = a.activation(y, y, ACT.Copy, scale=m.meta[:, bass.ds(from_end(j) * 2 + u, 1), M_SCALE])
                last.then_inc(y_ready.sem, 1)

            staged(a, CHUNKS, 2, (2, normalise), (1, transposed), (3, root), (4, features), (0, scale))

        @block.tensor
        def _(pe):
            pe.sem_inc(hgT_ps.sem, hgT_ps.ahead)
            pe.sem_inc(out_ps.sem, out_ps.ahead)

            def turn_x(j, q, turn):
                pe.wait_ge(xc_ready.sem, xc_ready.done(j))
                pe.wait_ge(xp_ready, j)
                for u in range(2):
                    for h in range(2):
                        last = pe.transpose(ps[:, 0, u * D + h * P:u * D + h * P + P], xc[:, h, u * P:u * P + P], m.ident[:, :])
                last.then_inc(x_ps, 1)

            def turn_h(j, q, turn):
                pe.wait_ge(h_ready.sem, h_ready.done(j))
                pe.wait_ge(g_ready.sem, g_ready.done(j))
                pe.wait_ge(hgT_ready.sem, hgT_ready.free(j, 1))
                for s in range(2):
                    for kh in range(2):
                        for u in range(2):
                            last = pe.transpose(ps[:, 1 + s, kh * CW + u * P:kh * CW + u * P + P],
                                                hg[:, q, s, u, kh * P:kh * P + P], m.ident[:, :])
                last.then_inc(hgT_ps.sem, 1)

            def products(j, q, turn):
                pe.wait_ge(hgT_ready.sem, hgT_ready.done(j))
                pe.wait_ge(out_ready.sem, out_ready.free(j, 2))
                for s, w in enumerate((m.upd, m.msg)):
                    for u in range(2):
                        for kh in range(2):
                            last = pe.matmul(ps[:, 3 + 2 * q + s, u * D:u * D + D], hgT[:, q, s, kh, u * P:u * P + P], w[:, kh, :],
                                             start=(kh == 0), stop=(kh == 1))
                last.then_inc(out_ps.sem, 1)

            staged(pe, CHUNKS, 2, (1, turn_h), (3, turn_x), (0, products))

        @block.vector
        def _(v):
            chain = Chain(v, dve_own)
            v.sem_inc(out_ready.sem, out_ready.ahead)
            back.init(v)
            v.tensor_tensor(m.meta[:, :, M_SCALE], m.meta[:, :, M_SCALE], m.gates[:, :], ALU.mult).then_inc(scales_ready, 1)

            def fill(j, q, turn):
                back.fill(v, j, q % 2)

            def back_scan(j, q, turn):
                back.scan(v, j, q % 2)

            def keep_carry(j, q, turn):
                back.keep_carry(v, j, q % 2)

            def statistics(j, q, turn):
                v.wait_ge(x_ps, j + 1)
                v.wait_ge(loaded[q], (turn + 1) * 32)
                v.wait_ge(h_ready.sem, h_ready.free(j, 2))
                v.wait_ge(xb_ready.sem, xb_ready.free(j, 2))
                v.tensor_tensor(xp[:, q % 2, :, :], ps[:, 0, :].rearrange("p (u k) -> p u k", u=2), ld[:, q, :, 0:D], ALU.add).then_inc(xp_ready, 1)
                v.wait_ge(xp_ready, j + 1)
                for u in range(2):
                    last = v.bn_stats(stats[:, u, :], xp[:, q % 2, u, :])
                last.then_inc(stats_ready, 1)

            def aggregate(j, q, turn):
                v.wait_ge(stats_ready, j + 1)
                settle(v, m)
                for u in range(2):
                    last = v.bn_aggr(mv[:, u, :], stats[:, u, :])
                last.then_inc(mv_ready, 1)

            def scales(j, q, turn):
                v.wait_ge(std_ready, j + 1)
                v.wait_ge(h_ready.sem, h_ready.free(j, 1))
                chain(v.reciprocal(rstd[:, :], std[:, :]))
                v.scalar_tensor_tensor(nmr[:, :], mv[:, :, 0], -1.0, rstd[:, :], ALU.mult, ALU.mult).then_inc(ln_ready, 1)

            def results(j, q, turn):
                half, slot, q = q // 2, q, q % 2
                v.wait_ge(out_ps.sem, out_ps.done(j))
                v.wait_ge(xb_ready.sem, xb_ready.done(j))
                v.wait_ge(y_ready.sem, y_ready.free(j, 2))
                v.wait_ge(stored[q], (turn * (LD // 2) + half) * 16)
                v.wait_ge(rewritten[(slot - 2) % LD], (turn + slot // 2) * 32)
                v.tensor_tensor(res[:, q, 0, :, :], ps[:, 3 + 2 * q, :].rearrange("p (u k) -> p u k", u=2), xb[:, slot, :, :], ALU.add)
                for u in range(2):
                    v.tensor_tensor(res[:, q, 1, u, :], ps[:, 4 + 2 * q, u * D:u * D + D], m.msgb[:, :], ALU.add)
                v.tensor_copy(rewrite_to[:, q, :], m.last_src[:, bass.ds(from_end(j) * 2, 2)]).then_inc(out_ready.sem, 1)

            staged(v, CHUNKS, LD, (2, scales), (3, statistics), (4, back_scan), (3, aggregate), (4, keep_carry), (5, fill), (0, results),
                   chain=chain, counts=(1, 0, 0, 0, 0, 0, 0))


def all_nodes(nc, m):
    sb, ps = m.sb, m.psum
    sem = lambda n: m.sem(f"{n}_d")
    G = 4
    ROWS = G * P
    TURNS = -(-N // ROWS)
    XS = 6
    xs = sb("xs", [P, XS, G, D], F32)
    h = sb("h_d", [P, 3, G, D], F32)
    used_up = m.wt.rearrange("p l s k o -> p (l s k o)")
    hT = used_up[:, 0:2 * G * D].rearrange("p (q g k) -> p q g k", q=2, g=G)
    cb = used_up[:, 2 * G * D:2 * G * D + 2 * 2 * D].rearrange("p (w g k) -> p w g k", w=2, g=2)
    diag = sb("diag_d", [P, 2, P], F32)
    stats = sb("stats_d", [P, G, 6], F32)
    mv = sb("mv_d", [P, 2, G, 2], F32)
    std = sb("std_d", [P, G], F32)
    rstd = sb("rstd_d", [P, 2, G], F32)
    nmr = sb("nmr_d", [P, 2, G], F32)
    c_ready, c_ps, cb_ready, mv_ready, std_ready, ln_ready, dve_own = (
        sem(n) for n in ("c_ready", "c_ps", "cb_ready", "mv_ready", "std_ready", "ln_ready", "dve_own"))
    xp_ready, xb_ready, hT_ready, res_ready, h_ready, out_ps = (
        Signal(sem(n), 1) for n in ("xp_ready", "xb_ready", "hT_ready", "res_ready", "h_ready", "out_ps"))
    hT_ps = Signal(sem("hT_ps"), 2)
    loaded = [sem(f"loaded{q}") for q in range(XS)]
    stored = [sem(f"stored{q}") for q in range(XS)]
    SLOTS = XS
    rel = [sb(f"rel{q}", [P, D + 1], F32) for q in range(SLOTS)]
    rel_of = sb("rel_of", [P, SLOTS], I32)
    rel_of_ready = sem("rel_of_ready")
    gate_kept = Signal(sem("gate_kept"), SLOTS - 1)
    rel_in = [sem(f"rel_in{q}") for q in range(SLOTS)]
    rel_out = [sem(f"rel_out{q}") for q in range(SLOTS)]

    def at(c):
        return N - ROWS if isinstance(c, int) and c == TURNS - 1 else c * ROWS

    with nc.Block() as block:
        @block.sync
        def _(sp):
            def load(c, q, turn):
                sp.wait_ge(stored[q], turn * 16)
                sp.dma_start(xs[:, q, :, :], m.x[bass.ds(at(c), ROWS), :].rearrange("(p g) k -> p g k", g=G)).then_inc(loaded[q], 16)

            def store(c, q, turn):
                if isinstance(c, int) and c == TURNS - 1:
                    sp.wait_ge(stored[(c - 1) % XS], ((c - 1) // XS + 1) * 16)
                sp.wait_ge(res_ready.sem, res_ready.done(c))
                sp.dma_start(m.out[bass.ds(at(c), ROWS), :].rearrange("(p g) k -> p g k", g=G), xs[:, q, :, :]).then_inc(stored[q], 16)

            def store_relations(t, q, turn):
                sp.wait_ge(rel_in[q], (turn + 1) * 16)
                sp.dma_start(m.relations[bass.ds(t * P, P), :], rel[q][:, 0:D]).then_inc(rel_out[q], 16)

            staged(sp, TURNS, SLOTS, (4, load), (0, store_relations), (0, store), peel=1)
            for t in range(TURNS, TILES):
                store_relations(t, t % SLOTS, t // SLOTS)
            for q in range(SLOTS):
                sp.wait_ge(rel_out[q], len(range(q, TILES, SLOTS)) * 16)
            for q in range(XS):
                sp.wait_ge(stored[q], len(range(q, TURNS, XS)) * 16)

        @block.gpsimd
        def _(g):
            g.sem_inc(xb_ready.sem, xb_ready.ahead)
            g.sem_inc(gate_kept.sem, gate_kept.ahead)
            g.wait_ge(cb_ready, 1)

            def bias(c, q, turn):
                g.wait_ge(xp_ready.sem, xp_ready.done(c))
                for b in range(2):
                    half = xs[:, q, 2 * b:2 * b + 2, :]
                    last = g.tensor_tensor(half, half, cb[:, 1, :, :], ALU.add)
                last.then_inc(xb_ready.sem, 1)

            def relations(t, q, turn):
                g.wait_ge(rel_out[q], turn * 16)
                g.wait_ge(gate_kept.sem, gate_kept.free(t, SLOTS))
                settle(g, m)
                g.tensor_copy(rel_of[:, q:q + 1], m.meta[:, bass.ds(t, 1), M_TYPE]).then_inc(rel_of_ready, 1)
                g.wait_ge(rel_of_ready, t + 1)
                settle(g, m)
                g.indirect_dma_start(out=rel[q][:, :], out_offset=None, in_=m.rel_table,
                                     in_offset=bass.IndirectOffsetOnAxis(ap=rel_of[:, q:q + 1], axis=0)).then_inc(rel_in[q], 16)

            def keep_gate(t, q, turn):
                g.wait_ge(rel_in[q], (turn + 1) * 16)
                settle(g, m)
                g.tensor_copy(m.gates[:, bass.ds(t, 1)], rel[q][:, D:D + 1]).then_inc(gate_kept.sem, 1)

            staged(g, TURNS, SLOTS, (2, bias), (2, relations), (0, keep_gate))
            for t in range(TURNS, TILES):
                relations(t, t % SLOTS, t // SLOTS)
                keep_gate(t, t % SLOTS, t // SLOTS)

        @block.scalar
        def _(a):
            a.sem_inc(hT_ready.sem, hT_ready.ahead)
            a.sem_inc(h_ready.sem, h_ready.ahead)
            for k in range(2):
                last = a.activation(diag[:, k, :], m.ident[:, :], ACT.Copy, scale=m.coef[:, 2, k:k + 1])
            last.then_inc(c_ready, 1)

            def normalise(c, q, turn):
                h_slot, q = q % 3, q % 2
                a.wait_ge(ln_ready, c + 1)
                for n in range(G):
                    row = h[:, h_slot, n, :]
                    last = a.activation(row, row, ACT.Relu, bias=nmr[:, q, n:n + 1], scale=rstd[:, q, n:n + 1])
                last.then_inc(h_ready.sem, 1)

            def transposed(c, q, turn):
                q = q % 2
                a.wait_ge(hT_ps.sem, hT_ps.done(c))
                a.wait_ge(out_ps.sem, out_ps.free(c, 2))
                for b in range(2):
                    last = a.activation(hT[:, q, 2 * b:2 * b + 2, :], ps[:, 2 * q + b, :].rearrange("p (g k) -> p g k", g=2), ACT.Copy)
                last.then_inc(hT_ready.sem, 1)

            def root(c, q, turn):
                a.wait_ge(mv_ready, c + 1)
                a.activation(std[:, :], mv[:, q % 2, :, 1], ACT.Sqrt, bias=m.eps[:, :]).then_inc(std_ready, 1)

            staged(a, TURNS, SLOTS, (1, transposed), (2, normalise), (3, root))

        @block.tensor
        def _(pe):
            pe.sem_inc(hT_ps.sem, hT_ps.ahead)
            pe.sem_inc(out_ps.sem, out_ps.ahead)
            pe.wait_ge(c_ready, 1)
            pe.matmul(ps[:, 4, 0:D], m.ones[:, :], diag[:, :, :].rearrange("p h k -> p (h k)"), start=True, stop=True).then_inc(c_ps, 1)

            def turn_h(c, q, turn):
                h_slot, q = q % 3, q % 2
                pe.wait_ge(h_ready.sem, h_ready.done(c))
                pe.wait_ge(hT_ready.sem, hT_ready.free(c, 2))
                for n in range(G):
                    for kh in range(2):
                        last = pe.transpose(ps[:, 2 * q + n // 2, (n % 2) * D + kh * P:(n % 2) * D + kh * P + P],
                                            h[:, h_slot, n, kh * P:kh * P + P], m.ident[:, :])
                last.then_inc(hT_ps.sem, 1)

            def products(c, q, turn):
                q = q % 2
                pe.wait_ge(hT_ready.sem, hT_ready.done(c))
                pe.wait_ge(res_ready.sem, res_ready.free(c, 2))
                for n in range(G):
                    for kh in range(2):
                        last = pe.matmul(ps[:, 4 + 2 * q + n // 2, (n % 2) * D:(n % 2) * D + D], hT[:, q, n, kh * P:kh * P + P],
                                         m.upd[:, kh, :], start=(kh == 0), stop=(kh == 1))
                last.then_inc(out_ps.sem, 1)

            pe.wait_ge(cb_ready, 1)
            staged(pe, TURNS, SLOTS, (1, turn_h), (0, products))

        @block.vector
        def _(v):
            chain = Chain(v, dve_own)
            v.sem_inc(xp_ready.sem, xp_ready.ahead)
            v.sem_inc(res_ready.sem, res_ready.ahead)
            v.wait_ge(c_ps, 1)
            for n in range(2):
                v.tensor_copy(cb[:, 0, n, :], ps[:, 4, 0:D])
                last = v.tensor_tensor(cb[:, 1, n, :], ps[:, 4, 0:D], m.updb[:, :], ALU.add)
            last.then_inc(cb_ready, 1)
            v.wait_ge(cb_ready, 1)

            def add_constant(c, q, turn):
                v.wait_ge(loaded[q], (turn + 1) * 16)
                v.wait_ge(hT_ps.sem, hT_ps.free(c, 3))
                xp = h[:, q % 3, :, :]
                for b in range(2):
                    last = v.tensor_tensor(xp[:, 2 * b:2 * b + 2, :], xs[:, q, 2 * b:2 * b + 2, :], cb[:, 0, :, :], ALU.add)
                last.then_inc(xp_ready.sem, 1)

            def statistics(c, q, turn):
                v.wait_ge(xp_ready.sem, xp_ready.done(c))
                xp, q = h[:, q % 3, :, :], q % 2
                for n in range(G):
                    last = v.bn_stats(stats[:, n, :], xp[:, n, :])
                chain(last)
                settle(v, m)
                for n in range(G):
                    last = v.bn_aggr(mv[:, q, n, :], stats[:, n, :])
                last.then_inc(mv_ready, 1)

            def scales(c, q, turn):
                q = q % 2
                v.wait_ge(h_ready.sem, h_ready.free(c, 2))
                v.wait_ge(std_ready, c + 1)
                chain(v.reciprocal(rstd[:, q, :], std[:, :]))
                v.scalar_tensor_tensor(nmr[:, q, :], mv[:, q, :, 0], -1.0, rstd[:, q, :], ALU.mult, ALU.mult).then_inc(ln_ready, 1)

            def results(c, q, turn):
                v.wait_ge(out_ps.sem, out_ps.done(c))
                v.wait_ge(xb_ready.sem, xb_ready.done(c))
                for b in range(2):
                    half = xs[:, q, 2 * b:2 * b + 2, :]
                    last = v.tensor_tensor(half, ps[:, 4 + 2 * (q % 2) + b, :].rearrange("p (g k) -> p g k", g=2), half, ALU.add)
                last.then_inc(res_ready.sem, 1)

            staged(v, TURNS, SLOTS, (2, scales), (3, add_constant), (3, statistics), (0, results), chain=chain, counts=(1, 0, 1, 0))


def add_messages(nc, m):
    sb, ps = m.sb, m.psum
    sem = lambda n: m.sem(f"{n}_a")
    GT = 5
    GROUPS = TILES // GT
    GW = GT * P
    BANKS = (GT + 1) // 2
    SLOTS = 2
    rows = m.big[:, 0:SLOTS * GT * D].rearrange("p (q u k) -> p q u k", q=SLOTS, u=GT)
    equal = m.big[:, 2560:2560 + SLOTS * GT * GW].rearrange("p (q u e) -> p q u e", q=SLOTS, u=GT)
    sums = m.big[:, 8960:8960 + SLOTS * GT * D].rearrange("p (q u k) -> p q u k", q=SLOTS, u=GT)
    keys = m.big[:, 11520:11520 + SLOTS * GW].rearrange("p (q e) -> p q e", q=SLOTS)
    junk = m.big[:, 12800:12800 + GT * GW].rearrange("p (u e) -> p u e", u=GT)
    turned = m.big[:, 16000:16000 + P]
    dsts = m.big[:, 16128:16128 + TILES]
    first_to = sb("first_to", [P, GW], BF16)
    before = sb("before_a", [P, SLOTS, GT], F32)
    idx = sb("idx_a", [P, SLOTS, GT], I32)
    dsts_ready, dst_ps, dst_ready, dst_out, dve_own = (
        sem(n) for n in ("dsts_ready", "dst_ps", "dst_ready", "dst_out", "dve_own"))
    equal_ready, idx_ready, sum_ps, sum_ready = (Signal(sem(n), 1) for n in ("equal_ready", "idx_ready", "sum_ps", "sum_ready"))
    added = [sem(f"added{q}") for q in range(SLOTS)]
    loaded = [sem(f"loaded{q}") for q in range(SLOTS)]
    keys_in = [sem(f"keys_in{q}") for q in range(SLOTS)]

    with nc.Block() as block:
        @block.sync
        def _(sp):
            def load(n, q, turn):
                sp.wait_ge(sum_ps.sem, sum_ps.free(n, SLOTS))
                settle(sp, m)
                sp.dma_start(rows[:, q, :, :], m.messages[bass.ds(n * GW, GW), :].rearrange("(u p) k -> p u k", p=P)).then_inc(loaded[q], 16)

            def load_keys(n, q, turn):
                sp.wait_ge(idx_ready.sem, idx_ready.free(n, SLOTS))
                settle(sp, m)
                sp.dma_start(keys[:, q, :], bass.AP(tensor=m.placed_dst.tensor, offset=n * GW, ap=[[0, P], [1, GW]])).then_inc(keys_in[q], 16)

            sp.wait_ge(dst_ready, 1)
            sp.dma_start(m.placed_dst.rearrange("(t p) -> t p", p=P), turned[0:TILES, :]).then_inc(dst_out, 16)
            sp.wait_ge(dst_out, 16)
            staged(sp, GROUPS, SLOTS, (0, load_keys), (0, load))

        @block.gpsimd
        def _(g):
            def add(n, q, turn):
                g.wait_ge(idx_ready.sem, idx_ready.done(n))
                g.wait_ge(sum_ready.sem, sum_ready.done(n))
                g.wait_ge(added[1 - q], (turn + q) * GT * 16)
                settle(g, m)
                for u in range(GT):
                    g.indirect_dma_start(out=m.out, out_offset=bass.IndirectOffsetOnAxis(ap=idx[:, q, u:u + 1], axis=0),
                                         in_=sums[:, q, u, :], in_offset=None, compute_op=ALU.add,
                                         bounds_check=N - 1, oob_is_err=False).then_inc(added[q], 16)

            staged(g, GROUPS, SLOTS, (0, add))
            for q in range(SLOTS):
                g.wait_ge(added[q], len(range(q, GROUPS, SLOTS)) * GT * 16)

        @block.scalar
        def _(a):
            a.sem_inc(sum_ready.sem, sum_ready.ahead)

            def copy_sums(n, q, turn):
                a.wait_ge(sum_ps.sem, sum_ps.done(n))
                a.wait_ge(added[q], turn * GT * 16)
                for b in range(0, GT, 2):
                    w = min(2, GT - b)
                    last = a.activation(sums[:, q, b:b + w, :], ps[:, BANKS * q + b // 2, 0:w * D].rearrange("p (u k) -> p u k", u=w), ACT.Copy)
                last.then_inc(sum_ready.sem, 1)

            staged(a, GROUPS, SLOTS, (0, copy_sums))

        @block.tensor
        def _(pe):
            pe.sem_inc(sum_ps.sem, sum_ps.ahead)
            pe.wait_ge(dsts_ready, 1)
            pe.transpose(ps[0:TILES, 7, 0:P], dsts[:, :], m.ident[:, :]).then_inc(dst_ps, 1)

            def sum_equal(n, q, turn):
                pe.wait_ge(equal_ready.sem, equal_ready.done(n))
                pe.wait_ge(loaded[q], (turn + 1) * 16)
                pe.wait_ge(sum_ready.sem, sum_ready.free(n, 2))
                for u in range(GT):
                    for w in range(u, GT):
                        last = pe.matmul(ps[:, BANKS * q + u // 2, (u % 2) * D:(u % 2) * D + D], equal[:, q, w, u * P:u * P + P],
                                         rows[:, q, w, :], start=(w == u), stop=(w == GT - 1))
                last.then_inc(sum_ps.sem, 1)

            staged(pe, GROUPS, SLOTS, (0, sum_equal))

        @block.vector
        def _(v):
            chain = Chain(v, dve_own)
            v.sem_inc(equal_ready.sem, equal_ready.ahead)
            v.sem_inc(idx_ready.sem, idx_ready.ahead)
            v.memset(first_to[:, 0:GW - P], 1.0)
            v.tensor_copy(first_to[:, GW - P:GW], m.earlier[:, 0, 0:P])
            chain(v.tensor_copy(dsts[:, :], m.meta[:, :, M_DST]))
            v.engine_nop().then_inc(dsts_ready, 1)
            v.wait_ge(dst_ps, 1)
            v.tensor_copy(turned[0:TILES, :], ps[0:TILES, 7, 0:P]).then_inc(dst_ready, 1)

            def edges(n, q, turn):
                v.wait_ge(keys_in[q], (turn + 1) * 16)
                v.wait_ge(sum_ps.sem, sum_ps.free(n, 2))
                for w in range(GT):
                    last = v.tensor_scalar(equal[:, q, w, 0:w * P + P], keys[:, q, 0:w * P + P], dsts[:, bass.ds(n * GT + w, 1)], None, ALU.is_equal)
                last.then_inc(equal_ready.sem, 1)
                for u in range(GT):
                    last = v.scalar_tensor_tensor(junk[:, u, 0:u * P + P], keys[:, q, 0:u * P + P], dsts[:, bass.ds(n * GT + u, 1)],
                                                  first_to[:, GW - P - u * P:GW], ALU.is_equal, ALU.mult, accum_out=before[:, q, u:u + 1])
                chain(last)
                chain(v.tensor_scalar(before[:, q, :], before[:, q, :], 0.0, float(2 * N), ALU.is_gt, ALU.mult))
                v.wait_ge(added[q], turn * GT * 16)
                settle(v, m)
                v.tensor_tensor(idx[:, q, :], before[:, q, :], dsts[:, bass.ds(n * GT, GT)], ALU.add).then_inc(idx_ready.sem, 1)

            staged(v, GROUPS, SLOTS, (0, edges), chain=chain, counts=(2,))


_INS = ['x', 'src', 'dst', 'edge_type_500', 'L0_gnn_thetas', 'L0_gnn_phis', 'L0_gnn_gammas', 'L0_gnn_betas',
        'L1_gnn_relation_emb', 'L1_gnn_msg_w', 'L1_gnn_msg_b', 'L1_gnn_upd_w', 'L1_gnn_upd_b', 'L1_gnn_gate_w', 'L1_gnn_gate_b']


def kernel(**inputs):
    import numpy as _np
    import concourse.bacc as _bacc
    from concourse import mybir as _mybir
    from concourse.bass_utils import run_bass_kernel_spmd as _run

    nc = _bacc.Bacc("TRN2", target_bir_lowering=False, num_devices=1)
    arrays, args = {}, []
    for name in _INS:
        a = _np.ascontiguousarray(inputs[name])
        arrays[f"in_{name}"] = a
        args.append(nc.dram_tensor(f"in_{name}", a.shape, _mybir.dt.from_np(a.dtype), kind="ExternalInput").ap())
    args.append(nc.dram_tensor("out_0", (N, D), _mybir.dt.float32, kind="ExternalOutput").ap())
    program(nc, *args)
    r = _run(nc, [arrays], core_ids=[0])
    return r.results[0]["out_0"]
```
